# Optimizing a Trainium2 kernel written in Bass

```python
import numpy as np
import jax
import jax.numpy as jnp

def _softmax(x, axis=-1):
    return jax.nn.softmax(x, axis=axis)

def _gelu(x):
    return jax.nn.gelu(x, approximate=True)

def _silu(x):
    return jax.nn.silu(x)

def _sigmoid(x):
    return jax.nn.sigmoid(x)

def _layernorm(x, axis=-1, eps=1e-05):
    m = jnp.mean(x, axis=axis, keepdims=True)
    v = jnp.var(x, axis=axis, keepdims=True)
    return (x - m) / jnp.sqrt(v + eps)

def _scatter_add(tgt, idx, src, axis=0):
    return tgt.at[idx].add(src)

def _segment_sum(src, seg, n):
    return jax.ops.segment_sum(src, seg, n)
kernel_name = 'mk_prb_d1_jaxref_r2_93728b'

def setup_inputs(seed: int=0):
    np.random.seed(seed)
    _w = jnp.asarray

    def _L0_attn_setup():
        import jax, jax.numpy as jnp
        import numpy as np
        D_MODEL = 512
        D_INNER = 512
        N_HEADS = 16
        HEAD_DIM = D_INNER // N_HEADS
        D_STATE = 16
        DT_RANK = 16
        CHUNK = 64
        PROJ = 2 * D_INNER + 2 * D_STATE * N_HEADS + DT_RANK

        def _forward(x, W_in, dt_W, dt_b, A_log, D_param, W_out, norm_w):
            B, S, _ = x.shape
            H, P, N, K = (N_HEADS, HEAD_DIM, D_STATE, CHUNK)
            proj = x @ W_in.T
            xp = proj[..., :D_INNER]
            z = proj[..., D_INNER:2 * D_INNER]
            o = 2 * D_INNER
            B_ssm = proj[..., o:o + N * H].reshape(B, S, H, N)
            C_ssm = proj[..., o + N * H:o + 2 * N * H].reshape(B, S, H, N)
            dt_low = proj[..., o + 2 * N * H:]
            dt = jax.nn.softplus(dt_low @ dt_W.T + dt_b)
            xp = xp.reshape(B, S, H, P)
            A = -jnp.exp(A_log)
            nC = S // K
            xc = xp.reshape(B, nC, K, H, P)
            dtc = dt.reshape(B, nC, K, H)
            Bc = B_ssm.reshape(B, nC, K, H, N)
            Cc = C_ssm.reshape(B, nC, K, H, N)
            dA = dtc * A
            dAcs = jnp.cumsum(dA, axis=2)
            Lm = jnp.exp(dAcs[:, :, :, None, :] - dAcs[:, :, None, :, :])
            causal = jnp.tril(jnp.ones((K, K), jnp.float32))
            Lm = Lm * causal[None, None, :, :, None]
            scores = jnp.einsum('bcihn,bcjhn->bcijh', Cc, Bc) * Lm * dtc[:, :, None, :, :]
            y_intra = jnp.einsum('bcijh,bcjhp->bcihp', scores, xc)
            decay_to_end = jnp.exp(dAcs[:, :, -1:, :] - dAcs)
            wx = (dtc * decay_to_end)[..., None] * xc
            chunk_state = jnp.einsum('bckhn,bckhp->bchnp', Bc, wx)
            chunk_decay = jnp.exp(dAcs[:, :, -1, :])

            def step(h, inp):
                d, s = inp
                return (d[:, :, None, None] * h + s, h)
            h0 = jnp.zeros((B, H, N, P), jnp.float32)
            _, h_states = jax.lax.scan(step, h0, (jnp.moveaxis(chunk_decay, 1, 0), jnp.moveaxis(chunk_state, 1, 0)))
            h_states = jnp.moveaxis(h_states, 0, 1)
            y_cross = jnp.einsum('bcthn,bchnp,bcth->bcthp', Cc, h_states, jnp.exp(dAcs))
            y = (y_intra + y_cross).reshape(B, S, H, P)
            y = y + xp * D_param[None, None, :, None]
            y = y.reshape(B, S, D_INNER)
            rms = jnp.sqrt(jnp.mean(y * y, axis=-1, keepdims=True) + 1e-06)
            y = y / rms * norm_w
            y = y * jax.nn.silu(z)
            return y @ W_out.T
        key = jax.random.key(seed)
        ks = jax.random.split(key, 6)
        B, S = (4, 2048)
        x = jax.random.normal(ks[0], (B, S, D_MODEL), jnp.float32)
        W_in = jax.random.normal(ks[1], (PROJ, D_MODEL), jnp.float32) * 0.02
        dt_W = jax.random.normal(ks[2], (N_HEADS, DT_RANK), jnp.float32) * 0.1
        dt_b = jax.random.normal(ks[3], (N_HEADS,), jnp.float32) * 0.1
        A_log = jnp.full((N_HEADS,), jnp.log(0.5), jnp.float32)
        D_param = jnp.ones((N_HEADS,), jnp.float32)
        W_out = jax.random.normal(ks[4], (D_MODEL, D_INNER), jnp.float32) * 0.02
        norm_w = jnp.ones((D_INNER,), jnp.float32)
        return dict(x=x, W_in=W_in, dt_W=dt_W, dt_b=dt_b, A_log=A_log, D_param=D_param, W_out=W_out, norm_w=norm_w)
    _L0_attn_in = _L0_attn_setup()

    def _L0_ffn_setup():
        import jax, jax.numpy as jnp
        import numpy as np
        DM, NEXPERTS, SETS, ESIZE = (512, 32, 4, 32)
        B, S = (2, 4096)
        key = jax.random.key(seed)
        ks = jax.random.split(key, 7)
        sc = 0.02
        return {'x': jax.random.normal(ks[0], (B, S, DM), jnp.float32), 'Wc': jax.random.normal(ks[1], (DM, NEXPERTS, SETS), jnp.float32) * sc, 'bc': jax.random.normal(ks[2], (NEXPERTS, SETS), jnp.float32) * sc, 'W1': jax.random.normal(ks[3], (NEXPERTS, SETS, DM, ESIZE), jnp.float32) * sc, 'b1': jax.random.normal(ks[4], (NEXPERTS, SETS, ESIZE), jnp.float32) * sc, 'W2': jax.random.normal(ks[5], (NEXPERTS, SETS, DM, ESIZE), jnp.float32) * sc, 'b2': jax.random.normal(ks[6], (NEXPERTS, SETS, DM), jnp.float32) * sc}
    _L0_ffn_in = _L0_ffn_setup()
    _d = {'L0_attn_x': _L0_attn_in['x'], 'L0_attn_W_in': _L0_attn_in['W_in'], 'L0_attn_dt_W': _L0_attn_in['dt_W'], 'L0_attn_dt_b': _L0_attn_in['dt_b'], 'L0_attn_A_log': _L0_attn_in['A_log'], 'L0_attn_D_param': _L0_attn_in['D_param'], 'L0_attn_W_out': _L0_attn_in['W_out'], 'L0_attn_norm_w': _L0_attn_in['norm_w'], 'L0_ffn_Wc': _L0_ffn_in['Wc'], 'L0_ffn_bc': _L0_ffn_in['bc'], 'L0_ffn_W1': _L0_ffn_in['W1'], 'L0_ffn_b1': _L0_ffn_in['b1'], 'L0_ffn_W2': _L0_ffn_in['W2'], 'L0_ffn_b2': _L0_ffn_in['b2']}
    _x0 = _d['L0_attn_x']
    _d['L0_attn_x'] = jax.random.normal(jax.random.fold_in(jax.random.key(seed), 1), (16, 1024, 512), dtype=_x0.dtype)
    del _x0
    return _d

def reference(L0_attn_x, L0_attn_W_in, L0_attn_dt_W, L0_attn_dt_b, L0_attn_A_log, L0_attn_D_param, L0_attn_W_out, L0_attn_norm_w, L0_ffn_Wc, L0_ffn_bc, L0_ffn_W1, L0_ffn_b1, L0_ffn_W2, L0_ffn_b2):

    def _L0_attn_ref(x, W_in, dt_W, dt_b, A_log, D_param, W_out, norm_w):
        import jax, jax.numpy as jnp
        import numpy as np
        D_MODEL = 512
        D_INNER = 512
        N_HEADS = 16
        HEAD_DIM = D_INNER // N_HEADS
        D_STATE = 16
        DT_RANK = 16
        CHUNK = 64
        PROJ = 2 * D_INNER + 2 * D_STATE * N_HEADS + DT_RANK

        def _forward(x, W_in, dt_W, dt_b, A_log, D_param, W_out, norm_w):
            B, S, _ = x.shape
            H, P, N, K = (N_HEADS, HEAD_DIM, D_STATE, CHUNK)
            proj = x @ W_in.T
            xp = proj[..., :D_INNER]
            z = proj[..., D_INNER:2 * D_INNER]
            o = 2 * D_INNER
            B_ssm = proj[..., o:o + N * H].reshape(B, S, H, N)
            C_ssm = proj[..., o + N * H:o + 2 * N * H].reshape(B, S, H, N)
            dt_low = proj[..., o + 2 * N * H:]
            dt = jax.nn.softplus(dt_low @ dt_W.T + dt_b)
            xp = xp.reshape(B, S, H, P)
            A = -jnp.exp(A_log)
            nC = S // K
            xc = xp.reshape(B, nC, K, H, P)
            dtc = dt.reshape(B, nC, K, H)
            Bc = B_ssm.reshape(B, nC, K, H, N)
            Cc = C_ssm.reshape(B, nC, K, H, N)
            dA = dtc * A
            dAcs = jnp.cumsum(dA, axis=2)
            Lm = jnp.exp(dAcs[:, :, :, None, :] - dAcs[:, :, None, :, :])
            causal = jnp.tril(jnp.ones((K, K), jnp.float32))
            Lm = Lm * causal[None, None, :, :, None]
            scores = jnp.einsum('bcihn,bcjhn->bcijh', Cc, Bc) * Lm * dtc[:, :, None, :, :]
            y_intra = jnp.einsum('bcijh,bcjhp->bcihp', scores, xc)
            decay_to_end = jnp.exp(dAcs[:, :, -1:, :] - dAcs)
            wx = (dtc * decay_to_end)[..., None] * xc
            chunk_state = jnp.einsum('bckhn,bckhp->bchnp', Bc, wx)
            chunk_decay = jnp.exp(dAcs[:, :, -1, :])

            def step(h, inp):
                d, s = inp
                return (d[:, :, None, None] * h + s, h)
            h0 = jnp.zeros((B, H, N, P), jnp.float32)
            _, h_states = jax.lax.scan(step, h0, (jnp.moveaxis(chunk_decay, 1, 0), jnp.moveaxis(chunk_state, 1, 0)))
            h_states = jnp.moveaxis(h_states, 0, 1)
            y_cross = jnp.einsum('bcthn,bchnp,bcth->bcthp', Cc, h_states, jnp.exp(dAcs))
            y = (y_intra + y_cross).reshape(B, S, H, P)
            y = y + xp * D_param[None, None, :, None]
            y = y.reshape(B, S, D_INNER)
            rms = jnp.sqrt(jnp.mean(y * y, axis=-1, keepdims=True) + 1e-06)
            y = y / rms * norm_w
            y = y * jax.nn.silu(z)
            return y @ W_out.T
        return _forward(x, W_in, dt_W, dt_b, A_log, D_param, W_out, norm_w)

    def _L0_ffn_ref(x, Wc, bc, W1, b1, W2, b2):
        import jax, jax.numpy as jnp
        import numpy as np
        DM, NEXPERTS, SETS, ESIZE = (512, 32, 4, 32)
        B, S = (2, 4096)
        b, s, d = x.shape
        g = Wc.shape[1]
        grouped = x.reshape(b, s // g, g, d)
        logits = jnp.einsum('bntd,des->bntes', grouped, Wc) + bc
        tie = jnp.linspace(0.0, 1e-06, g, dtype=x.dtype).reshape(-1, 1, 1)
        logits = logits + tie
        perm = (logits == jnp.max(logits, axis=-3, keepdims=True)).astype(x.dtype)
        permuted = jnp.einsum('bntd,bntes->bnesd', grouped, perm)
        inner = jax.nn.relu(jnp.einsum('bnesd,esdf->bnesf', permuted, W1) + b1)
        result_permuted = jnp.einsum('bnesf,esdf->bnesd', inner, W2) + b2
        result = jnp.einsum('bnesd,bntes->bntd', result_permuted, perm)
        return result.reshape(b, s, d)
    x = L0_attn_x
    xn = _layernorm(x, axis=-1)
    x = x + _L0_attn_ref(xn, L0_attn_W_in, L0_attn_dt_W, L0_attn_dt_b, L0_attn_A_log, L0_attn_D_param, L0_attn_W_out, L0_attn_norm_w) + _L0_ffn_ref(xn, L0_ffn_Wc, L0_ffn_bc, L0_ffn_W1, L0_ffn_b1, L0_ffn_W2, L0_ffn_b2)
    return x

_drawn_inputs = setup_inputs


def setup_inputs(seed=0):
    import zlib

    import numpy as np

    out = dict(_drawn_inputs(seed))
    spreads = {'L0_attn_A_log': (-0.6931471824645996, 0.2),
     'L0_attn_D_param': (1.0, 0.2),
     'L0_attn_norm_w': (1.0, 0.2)}
    factors = {}
    for name, (base, spread) in spreads.items():
        noise = np.random.default_rng([zlib.crc32(name.encode()), seed]).standard_normal(out[name].shape)
        drawn = base * np.exp(spread * noise) if base else spread * noise
        out[name] = jnp.asarray(drawn.astype(out[name].dtype))
    for name, factor in factors.items():
        out[name] = (out[name] * factor).astype(out[name].dtype)
    return out
```

```python
from contextlib import ExitStack

import numpy as np

import concourse.bass as bass
from concourse import mybir

F32 = mybir.dt.float32
F32R = mybir.dt.float32r
BF16 = mybir.dt.bfloat16
U32 = mybir.dt.uint32
ALU = mybir.AluOpType
ACT = mybir.ActivationFunctionType
AX_X = mybir.AxisListType.X

P = 128
BATCH, SEQ, D = 16, 1024, 512
TOK = BATCH * SEQ
KD = D // P
H, HD, NS, R = 16, 32, 16, 16
DI = H * HD
KI = DI // P
CH = 64
ST = 256
NST = TOK // ST
STB = SEQ // ST
HB = 8
NE, SETS, ES = 32, 4, 32
EX = NE * SETS
GRP = 32
NQ = EX // 4
LN_EPS, RMS_EPS = 1e-5, 1e-6
TIE = np.arange(GRP, dtype=np.float32) * (np.float32(1e-6) / np.float32(GRP - 1))

C_B, C_DT, C_C, C_L = 0, H * NS, H * NS + H, 2 * H * NS + H
TCOLS = C_L + EX

GB = 64
GT = GB * GRP // P
NGB = TOK // (GB * GRP)
SG = 32
STL = SG * GRP // P
NSB = TOK // (SG * GRP)


def wait(eng, sem, value):
    if not isinstance(value, int) or value > 0:
        eng.wait_ge(sem, value)


def attention_phase(nc, io, keep):
    with ExitStack() as ctx:
        def sb(name, shape, dt=F32):
            return ctx.enter_context(nc.sbuf_tensor(name, shape, dt))

        def sem(name):
            return ctx.enter_context(nc.semaphore(name))

        bank = [ctx.enter_context(nc.psum_tensor(f"a_bank{i}", [P, 512], F32)) for i in range(8)]
        XN_OUT, PROJ0, PROJ1, TBC, SC0, SC1, YB, MISC = range(8)

        wd = [sb(f"wd{n}", [P, KD, 2 * DI], F32R) for n in "hl"]
        wt = [sb(f"wt{n}", [P, KD, TCOLS], F32R) for n in "hl"]
        wo = [sb(f"wo{n}", [P, KI, D], F32R) for n in "hl"]
        stage = sb("stage", [P, 2, KI * D])
        wlow = sb("wlow", [R, D])
        dtw = sb("dtw", [R, H])
        ident = sb("a_ident", [P, P])
        umat = sb("umat", [P, P])
        wmat = sb("wmat", [P, 4])
        mask = sb("mask", [P, CH], U32)
        hsel = sb("hsel", [P, HB])
        hexp = sb("hexp", [H, 2, P])
        ones = sb("ones", [P, 1])
        inv_di = sb("inv_di", [P, 1])
        mhalf = sb("mhalf", [P, 1])
        ln_eps = sb("ln_eps", [P, 1])
        rms_eps = sb("rms_eps", [P, 1])
        tie = sb("tie", [P, 1])
        a_row = sb("a_row", [P, H])
        dtb_row = sb("dtb_row", [P, H])
        bc_row = sb("bc_row", [P, EX])
        dcol = sb("dcol", [P, KI])
        nwcol = sb("nwcol", [P, KI])
        x = sb("x", [P, 2 * STB, D])
        bst = sb("bst", [P, 2, 6])
        mv = sb("mv", [P, 2, 2])
        ve = sb("ve", [P, 2])
        xn = sb("xn", [P, 2, D])
        xnT = [[sb(f"xnT{n}{b}", [P, KD, ST], F32R) for n in "hl"] for b in range(2)]
        raw = sb("raw", [P, 2, 2, TCOLS])
        v = sb("v", [P, 2, H])
        relu = sb("relu", [P, 2, H])
        vabs = sb("vabs", [P, 2, H])
        ex = sb("ex", [P, 2, H])
        u1 = sb("u1", [P, 2, H])
        lnu = sb("lnu", [P, 2, H])
        rcu = sb("rcu", [P, 2, H])
        lost = sb("lost", [P, 2, H])
        dt = sb("dt", [P, 2, H])
        dA = sb("dA", [P, 2, H])
        e1 = sb("e1", [P, 2, H])
        e2 = sb("e2", [P, 2, H])
        logs = sb("logs", [H, 8])
        mg = sb("mg", [P, 2, 2, 8])
        lb = sb("lb", [P, 2, EX])
        gmax = sb("gmax", [P, ST // GRP])
        permT = sb("permT", [P, 2, ST], BF16)
        BT = sb("BT", [P, 2, P])
        cexp = sb("cexp", [P, 2, 2, HB, CH])
        MT = sb("MT", [P, H, P])
        xtok = sb("xtok", [P, DI])
        xT = sb("xT", [P, 2, KI, ST])
        sz = sb("sz", [P, 2, KI, ST])
        g = sb("g", [P, 2, 2, 2 * HD])
        gs = sb("gs", [P, 2, 2 * HD])
        yv = sb("yv", [P, KI, P])
        yz = sb("yz", [P, KI, P])
        sq = sb("sq", [P, KI, P])
        sq2 = sb("sq2", [P, 2, P])
        ysq = sb("ysq", [P, 2, P])
        yg = [sb(f"yg{n}", [P, 2, KI, P], F32R) for n in "hl"]
        ms = sb("ms", [P, 2])
        rms = sb("rms", [P, 2])
        res = sb("res", [P, 2, D])

        const_in = sem("const_in")
        w_in = [sem(f"w_in{i}") for i in range(2)]
        w_hi = sem("w_hi")
        w_lo = sem("w_lo")
        wdt_ps = sem("wdt_ps")
        zeroed = sem("zeroed")
        a_ready = sem("a_ready")
        x_in = [sem(f"x_in{i}") for i in range(2 * STB)]
        ln = sem("ln")
        ln_pool = sem("ln_pool")
        kept = sem("kept")
        xn_ready = sem("xn_ready")
        xnT_ps = sem("xnT_ps")
        xnT_hi = sem("xnT_hi")
        xnT_lo = sem("xnT_lo")
        tok_ps = sem("tok_ps")
        tok_raw = sem("tok_raw")
        sp = sem("sp")
        sp_act = sem("sp_act")
        small_ps = sem("small_ps")
        small_cp = sem("small_cp")
        dA_ready = sem("dA_ready")
        e2_ready = sem("e2_ready")
        mg_ps = sem("mg_ps")
        mg_ready = sem("mg_ready")
        scaled = sem("scaled")
        lbs = sem("lbs")
        lT_ps = sem("lT_ps")
        pm = sem("pm")
        pm_out = [sem(f"pm_out{i}") for i in range(2)]
        d_ps = sem("d_ps")
        d_cp = sem("d_cp")
        tbc_ps = sem("tbc_ps")
        bt_cp = sem("bt_cp")
        cexp_cp = sem("cexp_cp")
        tx_ps = sem("tx_ps")
        xtok_cp = sem("xtok_cp")
        sc_ps = sem("sc_ps")
        mt_cp = sem("mt_cp")
        st_ps = sem("st_ps")
        st_add = sem("st_add")
        g_ready = sem("g_ready")
        cross0 = sem("cross0")
        y_ps = sem("y_ps")
        yv_cp = sem("yv_cp")
        yz_cp = sem("yz_cp")
        sq_cp = sem("sq_cp")
        ysum = sem("ysum")
        yg_hi = sem("yg_hi")
        yg_lo = sem("yg_lo")
        rms_ps = sem("rms_ps")
        rms_cp = sem("rms_cp")
        rms_pool = sem("rms_pool")
        o_ps = sem("o_ps")
        res_cp = sem("res_cp")
        res_out = [sem(f"res_out{i}") for i in range(2)]

        x_dram = io["x"].rearrange("(t p) d -> t p d", p=P)
        part_dram = keep["part"].rearrange("(t p) d -> t p d", p=P)
        perm_dram = keep["permT"].rearrange("e (s t) -> s e t", t=ST)

        stages = []
        for k in range(0, KD, 2):
            stages.append((io["w_dz"][:, k:k + 2, :], [w[:, k:k + 2, :] for w in wd]))
        for k in range(0, KD, 2):
            stages.append((io["w_tok"][:, k:k + 2, :], None))
        stages.append((io["w_out"], [w[:, :, :] for w in wo]))

        def stage_view(n):
            src = stages[n][0]
            return stage[:, n % 2, 0:src.shape[1] * src.shape[2]].rearrange("p (k c) -> p k c", k=src.shape[1])

        def stage_parts(n):
            if stages[n][1] is not None:
                return [(stage_view(n), *stages[n][1])]
            k = 2 * (n - KD // 2)
            s = stage_view(n)
            nb = C_DT - C_B
            return [(s[:, :, 0:nb], *[w[:, k:k + 2, C_B:C_DT] for w in wt]),
                    (s[:, :, nb:], *[w[:, k:k + 2, C_C:TCOLS] for w in wt])]

        consts = [(ident, "ident"), (umat, "umat"), (wmat, "wmat"), (mask, "mask"), (hsel, "hsel"),
                  (hexp, "hexp"), (tie, "tie"), (dcol, "dcol"), (nwcol, "nwcol"), (wlow, "w_dtlow"), (dtw, "dt_wT")]
        rows = [(a_row, "a_log"), (dtb_row, "dt_b"), (bc_row, "bc")]
        NCONST = 16 * (len(consts) + len(rows))

        SP = 7

        def valid(b, q):
            return not isinstance(b, int) or 0 <= STB * b + q < NST

        def step_of(b, q):
            return STB * b + q, q % STB

        def run_steps(eng, body):
            for q in range(STB):
                body(0, q)
            with eng.Fori(1, BATCH - 1) as b:
                for q in range(STB):
                    body(b, q)
            for q in range(STB):
                body(BATCH - 1, q)
            for q in range(2):
                body(BATCH, q)

        block = ctx.enter_context(nc.Block())

        @block.sync
        def _(sync):
            for dst, name in consts:
                sync.dma_start(dst[:], io[name]).then_inc(const_in, 16)
            for dst, name in rows:
                sync.dma_start(dst[:], io[name].partition_broadcast(P)).then_inc(const_in, 16)
            for t in range(4):
                sync.dma_start(x[:, t, :], x_dram[t]).then_inc(x_in[t], 16)
            for n, (src, _) in enumerate(stages):
                if n >= 2:
                    sync.wait_ge(w_lo, n - 1)
                sync.dma_start(stage_view(n), src).then_inc(w_in[n % 2], 16)

            def body(b, q):
                s, place = step_of(b, q)
                for i in range(2):
                    if i == 1 and valid(b, q):
                        wait(sync, pm, 2 * s + 2)
                        sync.dma_start(perm_dram[s], permT[:, place % 2, :]).then_inc(pm_out[place % 2], 16)
                    if valid(b, q - 2):
                        wait(sync, res_cp, 2 * (s - 2) + i + 1)
                        sync.dma_start(part_dram[2 * (s - 2) + i], res[:, i, :]).then_inc(res_out[i], 16)
                    if valid(b, q + 2):
                        slot = (2 * (place + 2) + i) % (2 * STB)
                        sync.dma_start(x[:, slot, :], x_dram[2 * (s + 2) + i]).then_inc(x_in[slot], 16)

            run_steps(sync, body)
            for i in range(2):
                sync.wait_ge(res_out[i], 16 * NST)
                sync.wait_ge(pm_out[i], 16 * (NST // 2))

        @block.gpsimd
        def _(pool):
            nc.gpsimd.memset(MT[:], 0.0).then_inc(zeroed, 1)
            for col, value in ((ones, 1.0), (inv_di, 1.0 / DI), (mhalf, -0.5), (ln_eps, LN_EPS), (rms_eps, RMS_EPS)):
                nc.gpsimd.memset(col[:], value).then_inc(zeroed, 1)
            pool.wait_ge(const_in, NCONST)
            pool.wait_ge(a_ready, 1)
            nc.gpsimd.tensor_scalar(a_row[:], a_row[:], -1.0, 1.0, ALU.mult, ALU.mult).then_inc(a_ready, 1)
            pool.wait_ge(zeroed, 6)
            pool.wait_ge(a_ready, 2)

            def inv_std(n, j):
                wait(pool, ln, 2 * n + 2)
                wait(pool, xn_ready, n - 1)
                nc.gpsimd.tensor_tensor(ve[:, j:j + 1], mv[:, j, 1:2], ln_eps[:], ALU.add).then_inc(ln_pool, 1)
                wait(pool, ln_pool, 2 * n + 1)
                nc.gpsimd.tensor_tensor(mv[:, j, 1:2], ve[:, j:j + 1], mhalf[:], ALU.pow).then_inc(ln_pool, 1)
                wait(pool, ln_pool, 2 * n + 2)
                nc.gpsimd.tensor_copy(keep["stats"][:, n, :], mv[:, j, :]).then_inc(kept, 1)

            def y_sums(n, i):
                wait(pool, sq_cp, n + 1)
                nc.gpsimd.tensor_tensor(sq2[:], sq[:, 0:2, :], sq[:, 2:4, :], ALU.add).then_inc(ysum, 1)
                wait(pool, ysum, 2 * n + 1)
                wait(pool, rms_ps, n - 1)
                nc.gpsimd.tensor_tensor(ysq[:, i, :], sq2[:, 0, :], sq2[:, 1, :], ALU.add).then_inc(ysum, 1)

            def inv_rms(n, i):
                wait(pool, rms_cp, n + 1)
                wait(pool, res_cp, n - 1)
                nc.gpsimd.tensor_tensor(ms[:, i:i + 1], ms[:, i:i + 1], rms_eps[:], ALU.add).then_inc(rms_pool, 1)
                wait(pool, rms_pool, 2 * n + 1)
                nc.gpsimd.tensor_tensor(rms[:, i:i + 1], ms[:, i:i + 1], mhalf[:], ALU.pow).then_inc(rms_pool, 1)

            def body(b, q):
                s, place = step_of(b, q)
                par = place % 2
                if valid(b, q + 1):
                    inv_std(2 * (s + 1) + 1, 1)
                if valid(b, q - 2):
                    y_sums(2 * (s - 2) + 1, 1)
                    inv_rms(2 * (s - 2), 0)
                if valid(b, q):
                    def logits(i):
                        n = 2 * s + i
                        wait(pool, tok_raw, 2 * n + 2)
                        wait(pool, lT_ps, s)
                        nc.gpsimd.tensor_tensor(lb[:, i, :], raw[:, par, i, C_L:TCOLS], bc_row[:], ALU.add).then_inc(lbs, 1)
                        wait(pool, lbs, 4 * s + 2 * i + 1)
                        nc.gpsimd.tensor_tensor(lb[:, i, :], lb[:, i, :], tie[:].to_broadcast([P, EX]), ALU.add).then_inc(lbs, 1)
                    wait(pool, tok_raw, 4 * s + 3)
                    for i in range(2):
                        r = nc.gpsimd.tensor_tensor(v[:, i, :], raw[:, par, i, C_DT:C_C], dtb_row[:], ALU.add)
                    r.then_inc(sp, 1)
                    logits(0)
                    one = ones[:].unsqueeze(2).to_broadcast([P, 2, H])
                    wait(pool, sp_act, 5 * s + 3)
                    nc.gpsimd.tensor_tensor(u1[:], ex[:], one, ALU.add).then_inc(sp, 1)
                    wait(pool, sp, SP * s + 2)
                    nc.gpsimd.tensor_tensor(lost[:], u1[:], one, ALU.subtract).then_inc(sp, 1)
                    wait(pool, sp, SP * s + 3)
                    nc.gpsimd.tensor_tensor(lost[:], ex[:], lost[:], ALU.subtract).then_inc(sp, 1)
                    logits(1)
                    wait(pool, sp_act, 5 * s + 5)
                    wait(pool, sp, SP * s + 4)
                    nc.gpsimd.tensor_tensor(lost[:], lost[:], rcu[:], ALU.mult).then_inc(sp, 1)
                    nc.gpsimd.tensor_tensor(dt[:], relu[:], lnu[:], ALU.add).then_inc(sp, 1)
                    wait(pool, sp, SP * s + 6)
                    nc.gpsimd.tensor_tensor(dt[:], dt[:], lost[:], ALU.add).then_inc(sp, 1)
                    wait(pool, sp, SP * s + 7)
                    for i in range(2):
                        r = nc.gpsimd.tensor_tensor(dA[:, i, :], dt[:, i, :], a_row[:], ALU.mult)
                    r.then_inc(dA_ready, 1)
                if valid(b, q + 2):
                    inv_std(2 * (s + 2), 0)
                if valid(b, q - 1):
                    y_sums(2 * (s - 1), 0)
                if valid(b, q - 2):
                    inv_rms(2 * (s - 2) + 1, 1)
                if valid(b, q):
                    wait(pool, small_cp, 3 * s + 2)
                    nc.gpsimd.tensor_tensor(e2[:], e2[:], dt[:], ALU.mult).then_inc(e2_ready, 1)
                    wait(pool, e2_ready, s + 1)
                    for i in range(2):
                        for c0, e in ((C_C, e1), (C_B, e2)):
                            blk = raw[:, par, i, c0:c0 + H * NS].rearrange("p (h n) -> p h n", n=NS)
                            nc.gpsimd.tensor_tensor(blk, blk, e[:, i, :].unsqueeze(2).to_broadcast([P, H, NS]),
                                                    ALU.mult).then_inc(scaled, 1)

            for t in range(3):
                inv_std(t, t % 2)
            run_steps(pool, body)

        @block.scalar
        def _(act):
            nc.scalar.preload_act_table_set("natural_log_exp_and_others")
            act.wait_ge(const_in, NCONST)
            nc.scalar.activation(a_row[:], a_row[:], ACT.Exp).then_inc(a_ready, 1)
            for n in range(len(stages)):
                act.wait_ge(w_in[n % 2], 16 * (n // 2 + 1))
                for rawp, hi, lo in stage_parts(n):
                    last = nc.scalar.copy(hi, rawp)
                last.then_inc(w_hi, 1)
            act.wait_ge(wdt_ps, 1)
            nc.scalar.copy(wt[0][:, :, C_DT:C_C], bank[MISC][:, 0:KD * H].rearrange("p (k h) -> p k h", k=KD)).then_inc(w_hi, 1)

            def hi(n, b, i):
                wait(act, xnT_ps, n + 1)
                nc.scalar.copy(xnT[b][0][:, :, i * P:(i + 1) * P], bank[XN_OUT][:].rearrange("p (k t) -> p k t", k=KD)).then_inc(xnT_hi, 1)

            def scan_copies(n):
                wait(act, tbc_ps, n + 1)
                nc.scalar.copy(BT[:], bank[TBC][:, 0:2 * P].rearrange("p (f t) -> p f t", f=2)).then_inc(bt_cp, 1)
                wait(act, tx_ps, n + 1)
                nc.scalar.copy(xtok[:], bank[MISC][:]).then_inc(xtok_cp, 1)

            def y_tail(n, i):
                wait(act, yv_cp, 4 * n + 4)
                wait(act, ysum, 2 * n - 1)
                nc.scalar.activation(sq[:], yv[:], ACT.Square).then_inc(sq_cp, 1)
                wait(act, yz_cp, 4 * n + 4)
                wait(act, o_ps, n - 1)
                nc.scalar.copy(yg[0][:, i, :, :], yz[:]).then_inc(yg_hi, 1)

            def tok_copies(n, par, i):
                wait(act, tok_ps, 2 * n + 1)
                nc.scalar.copy(raw[:, par, i, 0:C_C], bank[PROJ0][:, 0:C_C]).then_inc(tok_raw, 1)
                wait(act, tok_ps, 2 * n + 2)
                nc.scalar.copy(raw[:, par, i, C_C:TCOLS], bank[PROJ1][:, 0:TCOLS - C_C]).then_inc(tok_raw, 1)

            def rms_copy(n, i, col):
                wait(act, rms_ps, n + 1)
                wait(act, rms_pool, 2 * n - 2)
                nc.scalar.copy(ms[:, i:i + 1], bank[MISC][:, col:col + 1]).then_inc(rms_cp, 1)

            def body(b, q):
                s, place = step_of(b, q)
                par = place % 2
                if valid(b, q + 1):
                    hi(2 * (s + 1), 1 - par, 0)
                if valid(b, q - 1):
                    scan_copies(2 * (s - 1))
                if valid(b, q):
                    tok_copies(2 * s, par, 0)
                if valid(b, q - 2):
                    rms_copy(2 * (s - 2), 0, 64)
                    y_tail(2 * (s - 2) + 1, 1)
                if valid(b, q):
                    tok_copies(2 * s + 1, par, 1)
                    nc.scalar.preload_act_table_set("natural_log_exp_and_others")
                    wait(act, sp, SP * s + 1)
                    nc.scalar.activation(vabs[:], v[:], ACT.Abs).then_inc(sp_act, 1)
                    nc.scalar.activation(relu[:], v[:], ACT.Relu).then_inc(sp_act, 1)
                    wait(act, sp_act, 5 * s + 1)
                    nc.scalar.activation(ex[:], vabs[:], ACT.Exp, scale=-1.0).then_inc(sp_act, 1)
                    wait(act, sp, SP * s + 2)
                    nc.scalar.activation(lnu[:], u1[:], ACT.Ln).then_inc(sp_act, 1)
                    wait(act, sp_act, 5 * s + 4)
                    nc.scalar.activation(rcu[:], lnu[:], ACT.Exp, scale=-1.0).then_inc(sp_act, 1)
                if valid(b, q + 1):
                    hi(2 * (s + 1) + 1, 1 - par, 1)
                if valid(b, q - 1):
                    scan_copies(2 * (s - 1) + 1)
                    y_tail(2 * (s - 1), 0)
                if valid(b, q):
                    wait(act, d_ps, 4 * s + 1)
                    nc.scalar.copy(xT[:, par, 0:2, :], bank[PROJ0][:].rearrange("p (m t) -> p m t", m=2)).then_inc(d_cp, 1)
                    wait(act, d_ps, 4 * s + 2)
                    nc.scalar.copy(xT[:, par, 2:4, :], bank[PROJ1][:].rearrange("p (m t) -> p m t", m=2)).then_inc(d_cp, 1)
                    wait(act, small_ps, s + 1)
                    wait(act, scaled, 4 * s)
                    u = bank[MISC][:, 0:2 * H].rearrange("p (i h) -> p i h", i=2)
                    nc.scalar.activation(e1[:], u, ACT.Exp).then_inc(small_cp, 1)
                    nc.scalar.activation(e2[:], u, ACT.Exp, scale=-1.0).then_inc(small_cp, 1)
                    nc.scalar.copy(logs[:], bank[MISC][0:H, 2 * H:2 * H + 8]).then_inc(small_cp, 1)
                if valid(b, q - 2):
                    rms_copy(2 * (s - 2) + 1, 1, 64)
                if valid(b, q):
                    wait(act, mg_ps, s + 1)
                    nc.scalar.activation(mg[:, par, :, :], bank[MISC][:, 0:16].rearrange("p (f c) -> p f c", f=2),
                                         ACT.Exp).then_inc(mg_ready, 1)
                    for j in range(2):
                        wait(act, d_ps, 4 * s + 3 + j)
                        nc.scalar.activation(sz[:, par, 2 * j:2 * j + 2, :],
                                             bank[PROJ0 + j][:].rearrange("p (m t) -> p m t", m=2), ACT.Silu).then_inc(d_cp, 1)

            for i in range(2):
                hi(i, 0, i)
            run_steps(act, body)

        @block.vector
        def _(dve):
            def stats(n, slot, j):
                wait(dve, x_in[slot[0]], 16 * (slot[1] + 1))
                wait(dve, kept, n - 1)
                wait(dve, xn_ready, n - 1)
                nc.vector.bn_stats(bst[:, j, :], x[:, slot[0], :]).then_inc(ln, 1)

            def finish_stats(n, j):
                nc.vector.bn_aggr(mv[:, j, :], bst[:, j, :]).then_inc(ln, 1)

            def normalize(n, slot, j):
                wait(dve, ln_pool, 2 * n + 2)
                wait(dve, xnT_ps, n - 1)
                nc.vector.tensor_scalar(xn[:, j, :], x[:, slot[0], :], mv[:, j, 0:1], mv[:, j, 1:2],
                                        ALU.subtract, ALU.mult).then_inc(xn_ready, 1)

            def lo(n, b, i):
                wait(dve, xnT_hi, n + 1)
                nc.vector.tensor_tensor(xnT[b][1][:, :, i * P:(i + 1) * P], bank[XN_OUT][:].rearrange("p (k t) -> p k t", k=KD),
                                        xnT[b][0][:, :, i * P:(i + 1) * P].bitcast(F32), ALU.subtract).then_inc(xnT_lo, 1)

            def expand_c(n):
                wait(dve, bt_cp, n + 1)
                for f in range(2):
                    src = bank[TBC][:, (2 + f) * P:(3 + f) * P].rearrange("p (c i) -> p c i", c=2)
                    nc.vector.tensor_tensor(cexp[:, f, :, :, :], src.unsqueeze(2).to_broadcast([P, 2, HB, CH]),
                                            hsel[:].unsqueeze(1).unsqueeze(3).to_broadcast([P, 2, HB, CH]),
                                            ALU.mult).then_inc(cexp_cp, 1)

            def mask_scores(n):
                dve.wait_ge(zeroed, 6)
                wait(dve, sc_ps, n + 1)
                for f in range(2):
                    for c in range(2):
                        rows_ = slice(c * CH, (c + 1) * CH)
                        nc.vector.copy_predicated(MT[rows_, f * HB:(f + 1) * HB, c * CH:(c + 1) * CH],
                                                  mask[rows_, :].unsqueeze(1).to_broadcast([CH, HB, CH]),
                                                  bank[SC0 + f][rows_, :].rearrange("p (h i) -> p h i", h=HB)).then_inc(mt_cp, 1)

            def y_lo(n, i):
                wait(dve, yg_hi, n + 1)
                nc.vector.tensor_tensor(yg[1][:, i, :, :], yz[:], yg[0][:, i, :, :].bitcast(F32), ALU.subtract).then_inc(yg_lo, 1)

            def residual(s2, i, slot):
                n = 2 * s2 + i
                wait(dve, o_ps, n + 1)
                wait(dve, rms_pool, 2 * n + 2)
                wait(dve, res_out[i], 16 * s2)
                nc.vector.scalar_tensor_tensor(res[:, i, :], bank[XN_OUT][:], rms[:, i:i + 1], x[:, slot, :],
                                               ALU.mult, ALU.add).then_inc(res_cp, 1)

            def states(n, i, p0, nxt):
                wait(dve, st_ps, n + 1)
                wait(dve, g_ready, 4 * n + 4)
                nc.vector.tensor_tensor(gs[:], bank[TBC][:, 0:P].rearrange("p (f c) -> p f c", f=2), g[:, 0, :, :],
                                        ALU.add).then_inc(st_add, 1)
                wait(dve, st_add, 2 * n + 1)
                wait(dve, y_ps, n)
                for f in range(2):
                    nc.vector.tensor_scalar(g[:, 1, f, :], gs[:, f, :], mg[:, p0, f, 4 * i + 1:4 * i + 2],
                                            mg[:, p0, f, 4 * i + 2:4 * i + 3], ALU.mult, ALU.mult).then_inc(g_ready, 1)
                wait(dve, g_ready, 4 * n + 6)
                nc.vector.tensor_tensor(gs[:], bank[MISC][:, 0:P].rearrange("p (f c) -> p f c", f=2), g[:, 1, :, :],
                                        ALU.add).then_inc(st_add, 1)
                wait(dve, st_add, 2 * n + 2)
                wait(dve, cross0, n + 1)
                for f in range(2):
                    if nxt is None:
                        nc.vector.memset(g[:, 0, f, :], 0.0).then_inc(g_ready, 1)
                    else:
                        nc.vector.tensor_scalar(g[:, 0, f, :], gs[:, f, :], mg[:, p0, f, 4 * i + 3:4 * i + 4],
                                                mg[:, nxt[0], f, nxt[1]:nxt[1] + 1], ALU.mult, ALU.mult).then_inc(g_ready, 1)

            def gate(n, i, par):
                tt = slice(i * P, (i + 1) * P)
                wait(dve, y_ps, n + 1)
                wait(dve, sq_cp, n)
                for m in range(KI):
                    nc.vector.scalar_tensor_tensor(yv[:, m, :], xT[:, par, m, tt], dcol[:, m:m + 1],
                                                   bank[YB][:, m * P:(m + 1) * P], ALU.mult, ALU.add).then_inc(yv_cp, 1)
                wait(dve, yv_cp, 4 * n + 4)
                wait(dve, yg_lo, n)
                for m in range(KI):
                    nc.vector.scalar_tensor_tensor(yz[:, m, :], yv[:, m, :], nwcol[:, m:m + 1], sz[:, par, m, tt],
                                                   ALU.mult, ALU.mult).then_inc(yz_cp, 1)

            def picks(s, par, count):
                wait(dve, lT_ps, s + 1)
                lt = bank[TBC][:, 0:ST].rearrange("p (g t) -> p g t", t=GRP)
                nc.vector.tensor_reduce(gmax[:], lt, AX_X, ALU.max).then_inc(pm, 1)
                wait(dve, pm, 2 * s + 1)
                wait(dve, pm_out[par], 16 * count)
                nc.vector.tensor_tensor(permT[:, par, :].rearrange("p (g t) -> p g t", t=GRP), lt,
                                        gmax[:].unsqueeze(2).to_broadcast([P, ST // GRP, GRP]), ALU.is_equal).then_inc(pm, 1)

            def body(b, q):
                s, place = step_of(b, q)
                par = place % 2

                def slot(dq, i):
                    qq = q + dq
                    return ((2 * qq + i) % (2 * STB), b + qq // STB)

                for i in range(2):
                    nxt_tile = (1, 1) if i == 0 else (2, 0)
                    more = valid(b, q + nxt_tile[0])
                    n_next = 2 * (s + nxt_tile[0]) + nxt_tile[1]
                    if more:
                        stats(n_next, slot(*nxt_tile), nxt_tile[1])
                        wait(dve, ln, 2 * n_next + 1)
                    if valid(b, q + 1):
                        lo(2 * (s + 1) + i, 1 - par, i)
                    if more:
                        finish_stats(n_next, nxt_tile[1])
                    if valid(b, q - 1):
                        expand_c(2 * (s - 1) + i)
                    if i == 1 and valid(b, q - 1):
                        y_lo(2 * (s - 1), 0)
                    if more:
                        normalize(n_next, slot(*nxt_tile), nxt_tile[1])
                    if i == 1 and valid(b, q):
                        half = b * (STB // 2) + q // 2
                        picks(s, par, half)
                    if valid(b, q - 1):
                        mask_scores(2 * (s - 1) + i)
                    if i == 0 and valid(b, q - 2):
                        y_lo(2 * (s - 2) + 1, 1)
                    if valid(b, q - 2):
                        residual(s - 2, i, slot(-2, i)[0])
                    if valid(b, q - 1):
                        if i == 0:
                            nxt = (1 - par, 4)
                        else:
                            if valid(b, q):
                                wait(dve, mg_ready, s + 1)
                            nxt = None if place == 0 or not valid(b, q) else (par, 0)
                        states(2 * (s - 1) + i, i, 1 - par, nxt)
                        gate(2 * (s - 1) + i, i, 1 - par)

            for f in range(2):
                nc.vector.memset(g[:, 0, f, :], 0.0).then_inc(g_ready, 1)
            for f in range(2):
                nc.vector.memset(g[:, 1, f, :], 0.0).then_inc(g_ready, 1)
            for n in range(len(stages)):
                dve.wait_ge(w_hi, n + 1)
                for rawp, hi, lo_ in stage_parts(n):
                    last = nc.vector.tensor_tensor(lo_, rawp, hi.bitcast(F32), ALU.subtract)
                last.then_inc(w_lo, 1)
            dve.wait_ge(w_hi, len(stages) + 1)
            nc.vector.tensor_tensor(wt[1][:, :, C_DT:C_C], bank[MISC][:, 0:KD * H].rearrange("p (k h) -> p k h", k=KD),
                                    wt[0][:, :, C_DT:C_C].bitcast(F32), ALU.subtract).then_inc(w_lo, 1)
            for t in range(2):
                stats(t, (t, 0), t)
                dve.wait_ge(ln, 2 * t + 1)
                finish_stats(t, t)
                normalize(t, (t, 0), t)
            for i in range(2):
                lo(i, 0, i)
                if i == 0:
                    stats(2, (2, 0), 0)
                    dve.wait_ge(ln, 5)
                    finish_stats(2, 0)
            normalize(2, (2, 0), 0)
            run_steps(dve, body)

        @block.tensor
        def _(pe):
            def split_mm(out, lhs, rhs, k, nk):
                for n, (a, c) in enumerate(((0, 0), (0, 1), (1, 0))):
                    last = nc.tensor.matmul(out, lhs[a], rhs[c], start=(k == 0 and n == 0), stop=(k == nk - 1 and n == 2))
                return last

            def transpose_xn(n, j, freed):
                wait(pe, xn_ready, n + 1)
                wait(pe, xnT_lo, n)
                wait(pe, res_cp, freed)
                for k in range(KD):
                    last = nc.tensor.transpose(bank[XN_OUT][:, k * P:(k + 1) * P], xn[:, j, k * P:(k + 1) * P], ident[:])
                last.then_inc(xnT_ps, 1)

            def transpose_bc(n, par, i):
                wait(pe, scaled, 2 * n + 2)
                if i == 0:
                    wait(pe, pm, n + 2)
                wait(pe, st_add, 2 * n)
                for f in range(2):
                    nc.tensor.transpose(bank[TBC][:, f * P:(f + 1) * P], raw[:, par, i, C_B + f * P:C_B + (f + 1) * P], ident[:])
                for f in range(2):
                    last = nc.tensor.transpose(bank[TBC][:, (2 + f) * P:(3 + f) * P], raw[:, par, i, C_C + f * P:C_C + (f + 1) * P], ident[:])
                last.then_inc(tbc_ps, 1)

            def transpose_x(n, s1, par, i):
                wait(pe, d_cp, 4 * s1 + 2)
                if i == 0:
                    wait(pe, mg_ready, s1 + 1)
                for m in range(KI):
                    last = nc.tensor.transpose(bank[MISC][:, m * P:(m + 1) * P], xT[:, par, m, i * P:(i + 1) * P], ident[:])
                last.then_inc(tx_ps, 1)

            def project_tokens(n, b, i, read, count):
                for half, (c0, c1) in enumerate(((0, C_C), (C_C, TCOLS))):
                    wait(pe, read, count - 1 + half)
                    for k in range(KD):
                        last = split_mm(bank[PROJ0 + half][:, 0:c1 - c0], [t[:, k, i * P:(i + 1) * P] for t in xnT[b]],
                                        [w[:, k, c0:c1] for w in wt], k, KD)
                    last.then_inc(tok_ps, 1)

            def project_features(b, j):
                for m in range(2):
                    f = (2 * j + m) * P
                    for k in range(KD):
                        last = split_mm(bank[PROJ0 + j % 2][:, m * ST:(m + 1) * ST], [w[:, k, f:f + P] for w in wd],
                                        [t[:, k, :] for t in xnT[b]], k, KD)
                last.then_inc(d_ps, 1)

            def sum_squares(n, i):
                wait(pe, ysum, 2 * n + 2)
                nc.tensor.matmul(bank[MISC][:, 64:65], ysq[:, i, :], inv_di[:], start=True, stop=True).then_inc(rms_ps, 1)

            def scores(n):
                wait(pe, bt_cp, n + 1)
                wait(pe, cexp_cp, 2 * n + 2)
                for f in range(2):
                    for c in range(2):
                        last = nc.tensor.matmul(bank[SC0 + f][c * CH:(c + 1) * CH, :], BT[:, f, c * CH:(c + 1) * CH],
                                                cexp[:, f, c, :, :], start=True, stop=True)
                last.then_inc(sc_ps, 1)

            def project_out(n, i):
                wait(pe, yg_lo, n + 1)
                for k in range(KI):
                    last = split_mm(bank[XN_OUT][:], [y[:, i, k, :] for y in yg], [w[:, k, :] for w in wo], k, KI)
                last.then_inc(o_ps, 1)

            def chunk_states(n, par, i):
                for c in range(2):
                    rows_ = slice(c * CH, (c + 1) * CH)
                    for p in range(H // 2):
                        f, j = p // 4, p % 4
                        last = nc.tensor.matmul(bank[(TBC, MISC)[c]][32 * j:32 * j + 32, f * 64:(f + 1) * 64],
                                                raw[rows_, par, i, C_B + 32 * p:C_B + 32 * p + 32],
                                                xtok[rows_, 64 * p:64 * p + 64], start=True, stop=True)
                last.then_inc(st_ps, 1)

            def scan(n, par, i):
                wait(pe, xtok_cp, n + 1)
                wait(pe, mt_cp, 4 * n + 4)
                wait(pe, yv_cp, 4 * n)
                for h in range(H):
                    if h == 4:
                        chunk_states(n, par, i)
                    rows_ = slice(32 * (h % 4), 32 * (h % 4) + 32)
                    nc.tensor.matmul(bank[YB][rows_, (h // 4) * P:(h // 4 + 1) * P], xtok[:, HD * h:HD * (h + 1)], MT[:, h, :],
                                     start=(h < 4), stop=False, skip_group_check=True)
                for c in range(2):
                    wait(pe, g_ready, 4 * n + 4 + 2 * c)
                    for h in range(H):
                        rows_ = slice(32 * (h % 4), 32 * (h % 4) + 32)
                        col = (h // 4) * P + c * CH
                        last = nc.tensor.matmul(bank[YB][rows_, col:col + CH], g[:, c, h // HB, (h % 2) * HD:(h % 2 + 1) * HD],
                                                cexp[:, h // HB, c, h % HB, :], start=False, stop=(h >= H - 4),
                                                skip_group_check=True)
                    last.then_inc(cross0 if c == 0 else y_ps, 1)

            def body(b, q):
                s, place = step_of(b, q)
                par = place % 2
                for i in range(2):
                    n1, n2 = 2 * (s - 1) + i, 2 * (s - 2) + i
                    if valid(b, q + 1):
                        transpose_xn(2 * (s + 1) + i, i, n2)
                    if valid(b, q - 1):
                        transpose_bc(n1, 1 - par, i)
                        transpose_x(n1, s - 1, 1 - par, i)
                    if i == 0:
                        if valid(b, q):
                            wait(pe, xnT_lo, 2 * s + 2)
                            project_tokens(2 * s, par, 0, d_cp, 4 * s)
                        if valid(b, q - 2):
                            if valid(b, q - 1):
                                wait(pe, xtok_cp, n1 + 1)
                            else:
                                wait(pe, st_add, 2 * n1)
                            sum_squares(n2, i)
                        if valid(b, q):
                            project_tokens(2 * s + 1, par, 1, tok_raw, 4 * s + 2)
                        if valid(b, q - 1):
                            scores(n1)
                        if valid(b, q - 2):
                            if valid(b, q + 1):
                                wait(pe, xnT_lo, 2 * (s + 1) + i + 1)
                            else:
                                wait(pe, res_cp, n2)
                            project_out(n2, i)
                    else:
                        if valid(b, q):
                            wait(pe, tok_raw, 4 * s + 3)
                            project_features(par, 0)
                            wait(pe, tok_raw, 4 * s + 4)
                            project_features(par, 1)
                        if valid(b, q - 1):
                            wait(pe, xtok_cp, n1 + 1)
                        if valid(b, q - 2):
                            if not valid(b, q - 1):
                                wait(pe, rms_cp, n2)
                            sum_squares(n2, i)
                        if valid(b, q):
                            wait(pe, dA_ready, s + 1)
                            nc.tensor.matmul(bank[MISC][:, 0:2 * H], umat[:], dA[:].rearrange("p i h -> p (i h)"), start=True, stop=True)
                            for t in range(2):
                                last = nc.tensor.matmul(bank[MISC][0:H, 2 * H + 4 * t:2 * H + 4 * t + 4], dA[:, t, :], wmat[:],
                                                        start=True, stop=True)
                            last.then_inc(small_ps, 1)
                            wait(pe, lbs, 4 * s + 4)
                            if valid(b, q - 1):
                                wait(pe, cexp_cp, 2 * n1 + 2)
                            for t in range(2):
                                last = nc.tensor.transpose(bank[TBC][:, t * P:(t + 1) * P], lb[:, t, :], ident[:])
                            last.then_inc(lT_ps, 1)
                        if valid(b, q - 1):
                            scores(n1)
                        if valid(b, q - 2):
                            if valid(b, q + 1):
                                wait(pe, xnT_lo, 2 * (s + 1) + i + 1)
                            else:
                                wait(pe, res_cp, n2)
                            project_out(n2, i)
                        if valid(b, q):
                            wait(pe, d_cp, 4 * s + 1)
                            project_features(par, 2)
                            wait(pe, small_cp, 3 * s + 3)
                            if valid(b, q - 2):
                                wait(pe, rms_cp, n2 + 1)
                            for f in range(2):
                                last = nc.tensor.matmul(bank[MISC][:, f * 8:(f + 1) * 8], hexp[:, f, :], logs[:], start=True, stop=True)
                            last.then_inc(mg_ps, 1)
                            wait(pe, d_cp, 4 * s + 2)
                            project_features(par, 3)
                    if valid(b, q - 1):
                        if i == 1 and valid(b, q):
                            wait(pe, pm, 2 * s + 2)
                            wait(pe, mg_ready, s + 1)
                        if valid(b, q - 2) and (i == 0 or not valid(b, q)):
                            wait(pe, rms_cp, n2 + 1)
                        scan(n1, 1 - par, i)

            pe.wait_ge(const_in, NCONST)
            for k in range(KD):
                last = nc.tensor.matmul(bank[MISC][:, k * H:(k + 1) * H], wlow[:, k * P:(k + 1) * P], dtw[:], start=True, stop=True)
            last.then_inc(wdt_ps, 1)
            for i in range(2):
                transpose_xn(i, i, 0)
            pe.wait_ge(w_lo, len(stages) + 1)
            pe.wait_ge(zeroed, 6)
            run_steps(pe, body)


def gather_phase(nc, io, keep):
    with ExitStack() as ctx:
        def sb(name, shape, dt=F32):
            return ctx.enter_context(nc.sbuf_tensor("g_" + name, shape, dt))

        def sem(name):
            return ctx.enter_context(nc.semaphore("g_" + name))

        pick_bank = [ctx.enter_context(nc.psum_tensor(f"g_pick{i}", [P, 512], F32)) for i in range(4)]
        acc_bank = [ctx.enter_context(nc.psum_tensor(f"g_acc{i}", [P, 512], F32)) for i in range(4)]
        GPT = P // GRP
        QB = NQ // 4

        w1 = sb("w1", [P, KD, EX, ES])
        b1 = sb("b1", [P, NQ])
        ident = sb("ident", [P, P], BF16)
        ident32 = sb("ident32", [P, P])
        permT = sb("permT", [P, GT, P], BF16)
        perm = sb("perm", [P, GT, EX, GPT], F32R)
        x = [sb(f"x{i}", [P, GT, P]) for i in range(2)]
        stat = sb("stat", [P, GT, 2])
        xh = sb("xh", [P, GT, P], F32R)
        xl = sb("xl", [P, GT, P], F32R)
        picked = [sb(f"picked{i}", [P, EX, GB]) for i in range(2)]
        inner = sb("inner", [P, 2, NQ, GB // 2])

        small_in = sem("small_in")
        w1_in = [sem(f"w1_in{k}") for k in range(KD)]
        x_in = [sem(f"x_in{i}") for i in range(2)]
        perm_in = sem("perm_in")
        zeroed = sem("zeroed")
        ident_ready = sem("ident_ready")
        stat_cp = sem("stat_cp")
        centred = sem("centred")
        xn_ready = sem("xn_ready")
        hi_ready = sem("hi_ready")
        lo_ready = sem("lo_ready")
        perm_ps = sem("perm_ps")
        perm_cp = [sem(f"perm_cp{i}") for i in range(2)]
        pick_ps = sem("pick_ps")
        pick_cp = [sem(f"pick_cp{i}") for i in range(2)]
        acc_ps = sem("acc_ps")
        acc_cp = [sem(f"acc_cp{i}") for i in range(2)]
        inner_out = sem("inner_out")

        x_dram = io["x"].rearrange("(b t p) (k c) -> b k p t c", p=P, t=GT, c=P)
        perm_dram = keep["permT"].rearrange("e (b t c) -> b e t c", t=GT, c=P)
        inner_dram = keep["inner"]

        def run_batches(eng, body):
            body(0, False)
            with eng.Fori(1, NGB - 1) as b:
                body(b, False)
            body(NGB - 1, True)

        block = ctx.enter_context(nc.Block())

        @block.sync
        def _(sync):
            def load_x(b, k):
                wait(sync, lo_ready, 2 * (4 * b + k - 1))
                sync.dma_start(x[k % 2][:], x_dram[b, k]).then_inc(x_in[k % 2], 16)

            sync.dma_start(permT[:], perm_dram[0]).then_inc(perm_in, 16)
            sync.dma_start(ident32[:], io["ident"]).then_inc(small_in, 16)
            sync.dma_start(b1[:], io["b1"]).then_inc(small_in, 16)
            sync.dma_start(x[0][:], x_dram[0, 0]).then_inc(x_in[0], 16)
            sync.dma_start(x[1][:], x_dram[0, 1]).then_inc(x_in[1], 16)
            for k in range(KD):
                sync.dma_start(w1[:, k, :, :], io["w1"][:, k, :, :]).then_inc(w1_in[k], 16)

            def body(b, last):
                if not last:
                    sync.wait_ge(perm_ps, b + 1)
                    sync.dma_start(permT[:], perm_dram[b + 1]).then_inc(perm_in, 16)
                load_x(b, 2)
                load_x(b, 3)
                if not last:
                    load_x(b + 1, 0)
                    load_x(b + 1, 1)

            run_batches(sync, body)
            sync.wait_ge(inner_out, 2 * 16 * NGB)

        @block.gpsimd
        def _(pool):
            nc.gpsimd.memset(perm[:].bitcast(F32), 0.0).then_inc(zeroed, 1)
            pool.wait_ge(zeroed, 1)

            def normalize(b, k):
                n = 4 * b + k
                if k == 0:
                    wait(pool, xn_ready, n)
                    nc.gpsimd.tensor_copy(stat[:], keep["stats"][:, GT * b:GT * b + GT, :]
                                          if isinstance(b, int) else keep["stats"][:, bass.ds(GT * b, GT), :]).then_inc(stat_cp, 1)
                    pool.wait_ge(stat_cp, b + 1)
                pool.wait_ge(x_in[k % 2], 16 * (2 * b + k // 2 + 1))
                mean, inv = (stat[:, :, j:j + 1].to_broadcast([P, GT, P]) for j in range(2))
                nc.gpsimd.tensor_tensor(x[k % 2][:], x[k % 2][:], mean, ALU.subtract).then_inc(centred, 1)
                pool.wait_ge(centred, n + 1)
                nc.gpsimd.tensor_tensor(x[k % 2][:], x[k % 2][:], inv, ALU.mult).then_inc(xn_ready, 1)

            def body(b, last):
                normalize(b, 2)
                normalize(b, 3)
                if not last:
                    normalize(b + 1, 0)
                    normalize(b + 1, 1)

            normalize(0, 0)
            normalize(0, 1)
            run_batches(pool, body)

        def tiles_of(h):
            return slice(h * GT // 2, (h + 1) * GT // 2)

        def quadrants(bank_index):
            for r in range(GPT):
                rows_ = slice(GRP * r, GRP * r + GRP)
                src = pick_bank[bank_index][:].bitcast(BF16).rearrange("p (t e) -> p t e", t=GT // 2)
                yield perm[rows_, tiles_of(bank_index), :, r], src[rows_, :, :]

        def picked_view(k, t):
            return picked[k % 2][:, :, GPT * t:GPT * t + GPT]

        def pick_view(t):
            return pick_bank[t % 4][:].rearrange("p (e n) -> p e n", n=GPT)

        def inner_view(q):
            return inner[:, :, q, :]

        def acc_view(q):
            return acc_bank[q // QB][:, (q % QB) * GB:(q % QB + 1) * GB].rearrange("p (h n) -> p h n", h=2)

        @block.scalar
        def _(act):
            nc.scalar.preload_act_table_set("natural_log_exp_and_others")

            def split_hi(b, k):
                n = 4 * b + k
                act.wait_ge(xn_ready, n + 1)
                for h in range(2):
                    if h == 0:
                        wait(act, pick_ps, 16 * n)
                    nc.scalar.copy(xh[:, tiles_of(h), :], x[k % 2][:, tiles_of(h), :]).then_inc(hi_ready, 1)

            def copy_picks(b):
                wait(act, perm_ps, b + 1)
                for dst, src in quadrants(0):
                    r = nc.scalar.copy(dst, src)
                r.then_inc(perm_cp[0], 1)

            def copy_picked(b, k):
                for t in range(0, GT, 2):
                    act.wait_ge(pick_ps, 16 * (4 * b + k) + t + 1)
                    nc.scalar.copy(picked_view(k, t), pick_view(t)).then_inc(pick_cp[0], 1)

            def apply_relu(b):
                wait(act, inner_out, 32 * b)
                for j in range(2):
                    act.wait_ge(acc_ps, 4 * b + j + 1)
                    for q in range(QB * j, QB * j + QB):
                        r = nc.scalar.activation(inner_view(q), acc_view(q), ACT.Relu, bias=b1[:, q:q + 1])
                    r.then_inc(acc_cp[0], 1)

            def store_inner(b):
                for i in range(2):
                    act.wait_ge(acc_cp[i], 2 * b + 2)
                for h in range(2):
                    act.dma_start(inner_dram[2 * b + h], inner[:, h, :, :]).then_inc(inner_out, 16)

            def body(b, last):
                copy_picked(b, 1)
                split_hi(b, 2)
                copy_picked(b, 2)
                split_hi(b, 3)
                copy_picked(b, 3)
                if not last:
                    copy_picks(b + 1)
                    split_hi(b + 1, 0)
                    copy_picked(b + 1, 0)
                    split_hi(b + 1, 1)
                apply_relu(b)
                store_inner(b)

            act.wait_ge(small_in, 32)
            nc.scalar.copy(ident[:], ident32[:]).then_inc(ident_ready, 1)
            act.wait_ge(zeroed, 1)
            copy_picks(0)
            split_hi(0, 0)
            copy_picked(0, 0)
            split_hi(0, 1)
            run_batches(act, body)

        @block.vector
        def _(dve):
            def split_lo(b, k):
                n = 4 * b + k
                for h in range(2):
                    dve.wait_ge(hi_ready, 2 * n + h + 1)
                    nc.vector.tensor_tensor(xl[:, tiles_of(h), :], x[k % 2][:, tiles_of(h), :],
                                            xh[:, tiles_of(h), :].bitcast(F32), ALU.subtract).then_inc(lo_ready, 1)

            def copy_picks(b):
                wait(dve, perm_ps, b + 1)
                for dst, src in quadrants(1):
                    r = nc.vector.tensor_copy(dst, src)
                r.then_inc(perm_cp[1], 1)

            def copy_picked(b, k):
                for t in range(1, GT, 2):
                    dve.wait_ge(pick_ps, 16 * (4 * b + k) + t + 1)
                    nc.vector.tensor_copy(picked_view(k, t), pick_view(t)).then_inc(pick_cp[1], 1)

            def apply_relu(b):
                wait(dve, inner_out, 32 * b)
                for j in range(2, 4):
                    dve.wait_ge(acc_ps, 4 * b + j + 1)
                    for q in range(QB * j, QB * j + QB):
                        r = nc.vector.tensor_scalar(inner_view(q), acc_view(q), b1[:, q:q + 1], 0.0, ALU.add, ALU.max)
                    r.then_inc(acc_cp[1], 1)

            def body(b, last):
                copy_picked(b, 1)
                split_lo(b, 2)
                copy_picked(b, 2)
                split_lo(b, 3)
                copy_picked(b, 3)
                if not last:
                    copy_picks(b + 1)
                    split_lo(b + 1, 0)
                    copy_picked(b + 1, 0)
                    split_lo(b + 1, 1)
                apply_relu(b)

            dve.wait_ge(small_in, 32)
            dve.wait_ge(zeroed, 1)
            copy_picks(0)
            split_lo(0, 0)
            copy_picked(0, 0)
            split_lo(0, 1)
            run_batches(dve, body)

        @block.tensor
        def _(pe):
            def transpose_picks(b, n):
                pe.wait_ge(perm_in, 16 * (b + 1))
                for i in range(2):
                    wait(pe, pick_cp[i], 8 * n)
                for t in range(GT):
                    dst = pick_bank[t // (GT // 2)][:].bitcast(BF16)
                    c = (t % (GT // 2)) * P
                    last = nc.tensor.transpose(dst[:, c:c + P], permT[:, t, :], ident[:])
                last.then_inc(perm_ps, 1)

            def pick(b, k):
                n = 4 * b + k
                if k == 0:
                    for i in range(2):
                        pe.wait_ge(perm_cp[i], b + 1)
                for t in range(GT):
                    if t % (GT // 2) == 0:
                        pe.wait_ge(lo_ready, 2 * n + t // (GT // 2) + 1)
                    wait(pe, pick_cp[t % 2], 8 * n + t // 2 - 1)
                    rhs = perm[:, t, :, :]
                    nc.tensor.matmul(pick_bank[t % 4][:], xh[:, t, :], rhs, start=True, stop=False)
                    nc.tensor.matmul(pick_bank[t % 4][:], xl[:, t, :], rhs, start=False, stop=True).then_inc(pick_ps, 1)

            def apply_w1(b, k):
                n = 4 * b + k
                if not isinstance(b, int) or b == 0:
                    pe.wait_ge(w1_in[k], 16)
                for i in range(2):
                    pe.wait_ge(pick_cp[i], 8 * (n + 1))
                for q in range(NQ):
                    j, c = q // QB, (q % QB) * GB
                    if k == 0 and q % QB == 0:
                        wait(pe, acc_cp[j // 2], 2 * b - 1 + j % 2)
                    for e in range(4):
                        last = nc.tensor.matmul(acc_bank[j][ES * e:ES * e + ES, c:c + GB], w1[:, k, 4 * q + e, :],
                                                picked[k % 2][:, 4 * q + e, :], start=(k == 0 and q % QB == 0),
                                                stop=(k == KD - 1), skip_group_check=True)
                    if k == KD - 1 and q % QB == QB - 1:
                        last.then_inc(acc_ps, 1)

            def body(b, last):
                pick(b, 1)
                apply_w1(b, 0)
                pick(b, 2)
                apply_w1(b, 1)
                pick(b, 3)
                if not last:
                    transpose_picks(b + 1, 4 * b + 4)
                apply_w1(b, 2)
                if not last:
                    pick(b + 1, 0)
                apply_w1(b, 3)

            pe.wait_ge(ident_ready, 1)
            transpose_picks(0, 0)
            pick(0, 0)
            run_batches(pe, body)


def scatter_phase(nc, io, keep):
    with ExitStack() as ctx:
        def sb(name, shape, dt=F32):
            return ctx.enter_context(nc.sbuf_tensor("s_" + name, shape, dt))

        def sem(name):
            return ctx.enter_context(nc.semaphore("s_" + name))

        w2_bank = [ctx.enter_context(nc.psum_tensor(f"s_w2_{i}", [P, 512], F32)) for i in range(4)]
        rt_bank = [ctx.enter_context(nc.psum_tensor(f"s_rt{i}", [P, 512], F32)) for i in range(2)]
        out_bank = [ctx.enter_context(nc.psum_tensor(f"s_sum{i}", [P, 512], F32)) for i in range(2)]
        GPT = P // GRP
        QG = NQ // STL
        STEPS = NSB * KD

        w2 = sb("w2", [P, NQ, D])
        b2 = sb("b2", [P, KD, EX])
        ident = sb("ident", [P, P])
        inner = [sb(f"inner{i}", [P, NQ, SG]) for i in range(2)]
        inner4 = [sb(f"inner4_{i}", [P, NQ, SG, 4]) for i in range(2)]
        permT = [sb(f"permT{i}", [P, SG * GRP], BF16) for i in range(2)]
        perm = [sb(f"perm{i}", [P, SG * GRP]) for i in range(2)]
        resT = [sb(f"resT{i}", [P, SG, EX]) for i in range(2)]
        res = sb("res", [P, 4, GPT, P])
        ones = sb("ones", [P, 1])
        part = [sb(f"part{i}", [P, STL, P]) for i in range(2)]
        out = [sb(f"out{i}", [P, STL, P]) for i in range(2)]

        small_in = sem("small_in")
        w2_first = [sem(f"w2_first{j}") for j in range(4)]
        w2_in = [sem(f"w2_in{k}") for k in range(KD)]
        inner_in = [sem(f"inner_in{i}") for i in range(2)]
        perm_in = [sem(f"perm_in{i}") for i in range(2)]
        part_in = [sem(f"part_in{i}") for i in range(2)]
        zeroed = sem("zeroed")
        inner_ready = sem("inner_ready")
        perm_ready = sem("perm_ready")
        w2_ps = sem("w2_ps")
        res_ready = sem("res_ready")
        res_ps = sem("res_ps")
        res_cp = sem("res_cp")
        out_ps = sem("out_ps")
        out_cp = sem("out_cp")
        out_done = [sem(f"out_done{i}") for i in range(2)]

        part_dram = keep["part"].rearrange("(b t p) (k c) -> b k p t c", p=P, t=STL, c=P)
        out_dram = io["out"].rearrange("(b t p) (k c) -> b k p t c", p=P, t=STL, c=P)
        perm_dram = keep["permT"].rearrange("e (b c) -> b e c", c=SG * GRP)

        def run_batches(eng, body):
            for i in range(2):
                body(0, i)
            with eng.Fori(1, NSB // 2 - 1) as pair:
                for i in range(2):
                    body(pair, i)
            for i in range(2):
                body(NSB // 2 - 1, i)

        def is_first(pair, i, k, steps=1):
            return isinstance(pair, int) and KD * (2 * pair + i) + k < steps

        def is_last(pair, i, batches):
            return isinstance(pair, int) and 2 * pair + i + batches >= NSB

        block = ctx.enter_context(nc.Block())

        @block.sync
        def _(sync):
            def load_part(b, k):
                sync.dma_start(part[k % 2][:], part_dram[b, k]).then_inc(part_in[k % 2], 16)

            def load_batch(b, i):
                sync.dma_start(inner[i][:], keep["inner"][b]).then_inc(inner_in[i], 16)
                sync.dma_start(permT[i][:], perm_dram[b]).then_inc(perm_in[i], 16)

            def store(b, k):
                sync.dma_start(out_dram[b, k], out[k % 2][:]).then_inc(out_done[k % 2], 16)

            sync.dma_start(inner[0][:], keep["inner"][0]).then_inc(inner_in[0], 16)
            for j in range(4):
                quads = slice(j * NQ // 4, (j + 1) * NQ // 4)
                sync.dma_start(w2[:, quads, 0:P], io["w2"][:, quads, 0:P]).then_inc(w2_first[j], 16)
                if j == 0:
                    sync.dma_start(ident[:], io["ident"]).then_inc(small_in, 16)
                    sync.dma_start(b2[:], io["b2"]).then_inc(small_in, 16)
            sync.dma_start(permT[0][:], perm_dram[0]).then_inc(perm_in[0], 16)
            for k in range(1, KD):
                sync.dma_start(w2[:, :, k * P:(k + 1) * P], io["w2"][:, :, k * P:(k + 1) * P]).then_inc(w2_in[k], 16)
            load_batch(1, 1)
            load_part(0, 0)
            load_part(0, 1)

            def body(pair, i):
                b = 2 * pair + i
                for k in range(KD):
                    if not is_first(pair, i, k):
                        sync.wait_ge(out_cp, 2 * (KD * b + k))
                        if k < KD - 1:
                            load_part(b, k + 1)
                        elif not is_last(pair, i, 1):
                            load_part(b + 1, 0)
                        store(*((b, k - 1) if k else (b - 1, KD - 1)))
                    if k == 1 and not is_last(pair, i, 2):
                        sync.wait_ge(inner_ready, b + 1)
                        sync.wait_ge(perm_ready, b + 1)
                        load_batch(b + 2, i)

            run_batches(sync, body)
            sync.wait_ge(out_cp, 2 * STEPS)
            store(NSB - 1, KD - 1)
            for i in range(2):
                sync.wait_ge(out_done[i], 16 * STEPS // 2)

        @block.gpsimd
        def _(pool):
            def spread(pair, i):
                b = 2 * pair + i
                wait(pool, perm_ready, b)
                pool.wait_ge(inner_in[i], 16 * (pair + 1))
                wait(pool, w2_ps, STL * KD * (b - 1))
                for e in range(4):
                    rows_ = slice(ES * e, ES * e + ES)
                    r = nc.gpsimd.tensor_tensor(inner4[i][rows_, :, :, e], inner[i][rows_, :, :],
                                                ones[rows_].unsqueeze(2).to_broadcast([ES, NQ, SG]), ALU.mult)
                r.then_inc(inner_ready, 1)
                pool.wait_ge(inner_ready, b + 1)
                pool.wait_ge(perm_in[i], 16 * (pair + 1))
                wait(pool, out_ps, STL * KD * (b - 1))
                nc.gpsimd.tensor_tensor(perm[i][:], permT[i][:], ones[:].to_broadcast([P, SG * GRP]), ALU.mult).then_inc(perm_ready, 1)

            def body(pair, i):
                if not is_last(pair, i, 1):
                    spread(*((pair, 1) if i == 0 else (pair + 1, 0)))

            nc.gpsimd.memset(ones[:], 1.0).then_inc(zeroed, 1)
            for i in range(2):
                nc.gpsimd.memset(inner4[i][:], 0.0).then_inc(zeroed, 1)
            pool.wait_ge(zeroed, 3)
            spread(0, 0)
            run_batches(pool, body)

        @block.scalar
        def _(act):
            def copy_results(m, t):
                act.wait_ge(res_ps, STL * m + t + 1)
                nc.scalar.copy(res[:, t % 4, :, :], rt_bank[t % 2][:].rearrange("p (n d) -> p n d", n=GPT)).then_inc(res_cp, 1)

            def body(pair, i):
                for k in range(KD):
                    if not is_first(pair, i, k):
                        for t in range(STL):
                            copy_results(KD * (2 * pair + i) + k - 1, t)

            run_batches(act, body)
            for t in range(STL):
                copy_results(STEPS - 1, t)

        @block.vector
        def _(dve):
            def add_b2(m, k, t):
                sets = slice(4 * QG * t, 4 * QG * (t + 1))
                dve.wait_ge(w2_ps, STL * m + t + 1)
                nc.vector.tensor_tensor(
                    resT[k % 2][:, :, sets].rearrange("p n (q e) -> p q n e", e=4),
                    w2_bank[t % 4][:].rearrange("p (q n e) -> p q n e", q=QG, e=4),
                    b2[:, k, sets].rearrange("p (q e) -> p q e", e=4).unsqueeze(2).to_broadcast([P, QG, SG, 4]),
                    ALU.add).then_inc(res_ready, 1)

            def write_out(b, m, k, h):
                use = 2 * b + k // 2
                tiles = slice(h * STL // 2, (h + 1) * STL // 2)
                dve.wait_ge(out_ps, STL * m + (h + 1) * STL // 2)
                dve.wait_ge(part_in[k % 2], 16 * (use + 1))
                wait(dve, out_done[k % 2], 16 * use)
                nc.vector.tensor_tensor(out[k % 2][:, tiles, :], out_bank[h][:].rearrange("p (t d) -> p t d", d=P),
                                        part[k % 2][:, tiles, :], ALU.add).then_inc(out_cp, 1)

            def body(pair, i):
                b = 2 * pair + i
                for k in range(KD):
                    m = KD * b + k
                    for t in range(STL):
                        add_b2(m, k, t)
                        if t == 0 and not is_first(pair, i, k, 2):
                            write_out(b, m - 2, k - 2, 1)
                        if t == STL // 2 and not is_first(pair, i, k):
                            write_out(b, m - 1, k - 1, 0)

            dve.wait_ge(small_in, 32)
            run_batches(dve, body)
            write_out(NSB, STEPS - 2, -2, 1)
            write_out(NSB, STEPS - 1, -1, 0)
            write_out(NSB, STEPS - 1, -1, 1)

        @block.tensor
        def _(pe):
            def apply_w2(m, k, t, i):
                wait(pe, res_ready, STL * m + t - 3)
                for j in range(QG):
                    q = QG * t + j
                    last = nc.tensor.matmul(w2_bank[t % 4][:, j * P:(j + 1) * P], w2[:, q, k * P:(k + 1) * P], inner4[i][:, q, :, :],
                                            start=True, stop=True)
                last.then_inc(w2_ps, 1)

            def transpose_results(m, k, t):
                if t == 0:
                    pe.wait_ge(res_ready, STL * (m + 1))
                wait(pe, res_cp, STL * m + t - 1)
                for g in range(GPT):
                    last = nc.tensor.transpose(rt_bank[t % 2][:, g * P:(g + 1) * P], resT[k % 2][:, GPT * t + g, :], ident[:])
                last.then_inc(res_ps, 1)

            def gather_results(b, m, i, k, t):
                h = t // (STL // 2)
                if k == 0 and t == 0:
                    pe.wait_ge(perm_ready, b + 1)
                pe.wait_ge(res_cp, STL * m + t + 1)
                if t % (STL // 2) == 0:
                    wait(pe, out_cp, 2 * m - 1 + h)
                c = (t % (STL // 2)) * P
                for g in range(GPT):
                    tok = (GPT * t + g) * GRP
                    last = nc.tensor.matmul(out_bank[h][GRP * g:GRP * g + GRP, c:c + P], perm[i][:, tok:tok + GRP],
                                            res[:, t % 4, g, :], start=True, stop=True)
                last.then_inc(out_ps, 1)

            def before(b, i, k, steps):
                return (b if k >= steps else b - 1), KD * b + k - steps, (i if k >= steps else 1 - i), (k - steps) % KD

            def finish(b, i, k, t, first2):
                if t > 0:
                    gather_results(*before(b, i, k, 1), t - 1)
                elif not first2:
                    gather_results(*before(b, i, k, 2), STL - 1)
                _, m1, _, k1 = before(b, i, k, 1)
                transpose_results(m1, k1, t)

            def body(pair, i):
                b = 2 * pair + i
                for k in range(KD):
                    if k == 0:
                        pe.wait_ge(inner_ready, b + 1)
                    if is_first(pair, i, k, KD) and k > 0:
                        pe.wait_ge(w2_in[k], 16)
                    for t in range(STL):
                        if is_first(pair, i, k) and t % (STL // 4) == 0:
                            pe.wait_ge(w2_first[t // (STL // 4)], 16)
                        apply_w2(KD * b + k, k, t, i)
                        if not is_first(pair, i, k):
                            finish(b, i, k, t, is_first(pair, i, k, 2))

            pe.wait_ge(small_in, 32)
            run_batches(pe, body)
            for t in range(STL):
                finish(NSB, 0, 0, t, False)
            gather_results(*before(NSB, 0, 0, 1), STL - 1)


def program(nc, io):
    with nc.sbuf_tensor("token_stats", [P, TOK // P, 2], F32) as stats:
        keep = dict(
            stats=stats,
            part=nc.dram_tensor("part_dram", [TOK, D], F32, kind="Internal").ap(),
            permT=nc.dram_tensor("permT_dram", [EX, TOK], BF16, kind="Internal").ap(),
            inner=nc.dram_tensor("inner_dram", [NSB, P, NQ, SG], F32, kind="Internal").ap(),
        )
        attention_phase(nc, io, keep)
        gather_phase(nc, io, keep)
        scatter_phase(nc, io, keep)


def layout(L0_attn_x, L0_attn_W_in, L0_attn_dt_W, L0_attn_dt_b, L0_attn_A_log, L0_attn_D_param, L0_attn_W_out,
           L0_attn_norm_w, L0_ffn_Wc, L0_ffn_bc, L0_ffn_W1, L0_ffn_b1, L0_ffn_W2, L0_ffn_b2):
    def blocks(w):
        return w.reshape(-1, P, w.shape[1]).transpose(1, 0, 2)

    nxz, nb = 2 * DI, H * NS
    tok_cols = np.concatenate([L0_attn_W_in[nxz:nxz + 2 * nb].T, L0_ffn_Wc.reshape(D, EX)], axis=1)
    tok = np.arange(P)
    same = tok[:, None] // CH == tok[None, :] // CH
    first = tok % CH == 0
    umat = same * ((tok[:, None] <= tok[None, :]) - 0.5 * first[:, None] - 0.5)
    wmat = np.stack([(tok // CH == c) * (0.5 + sign * 0.5 * first) for c in range(2) for sign in (1, -1)], axis=1)
    hexp = np.zeros((H, 2, P))
    for h in range(H):
        hexp[h, h // HB, NS * (h % HB):NS * (h % HB + 1)] = 1
    return dict(
        x=L0_attn_x.reshape(-1, D),
        w_dz=blocks(L0_attn_W_in[:nxz].T),
        w_tok=blocks(tok_cols),
        w_out=blocks(L0_attn_W_out.T),
        w_dtlow=L0_attn_W_in[nxz + 2 * nb:],
        dt_wT=L0_attn_dt_W.T,
        a_log=L0_attn_A_log, dt_b=L0_attn_dt_b, bc=L0_ffn_bc.reshape(EX),
        dcol=np.repeat(L0_attn_D_param, HD).reshape(KI, P).T,
        nwcol=L0_attn_norm_w.reshape(KI, P).T,
        w1=L0_ffn_W1.reshape(EX, KD, P, ES).transpose(2, 1, 0, 3),
        b1=L0_ffn_b1.reshape(NQ, 4, ES).transpose(1, 2, 0).reshape(P, NQ),
        w2=L0_ffn_W2.reshape(NQ, 4, D, ES).transpose(1, 3, 0, 2).reshape(P, NQ, D),
        b2=L0_ffn_b2.reshape(EX, KD, P).transpose(2, 1, 0),
        ident=np.eye(P, dtype=np.float32),
        umat=umat.astype(np.float32), wmat=wmat.astype(np.float32),
        mask=(np.arange(CH)[None, :] >= (tok % CH)[:, None]).astype(np.uint32),
        hsel=(tok[:, None] // NS == np.arange(HB)[None, :]).astype(np.float32),
        hexp=hexp.astype(np.float32),
        tie=TIE[tok % GRP].reshape(P, 1),
    )


def kernel(**inputs):
    import concourse.bacc as bacc
    from concourse.bass_utils import run_bass_kernel_spmd

    nc = bacc.Bacc("TRN2", target_bir_lowering=False, num_devices=1)
    arrays, io = {}, {}
    for name, a in layout(**{n: np.asarray(a) for n, a in inputs.items()}).items():
        a = np.ascontiguousarray(a)
        arrays[f"in_{name}_dram"] = a
        io[name] = nc.dram_tensor(f"in_{name}_dram", a.shape, mybir.dt.from_np(a.dtype), kind="ExternalInput").ap()
    io["out"] = nc.dram_tensor("out_0_dram", (TOK, D), F32, kind="ExternalOutput").ap()
    program(nc, io)
    result = run_bass_kernel_spmd(nc, [arrays], core_ids=[0])
    return result.results[0]["out_0_dram"].reshape(BATCH, SEQ, D)
```

```python
from contextlib import ExitStack

import numpy as np

import concourse.bass as bass
from concourse import mybir

F32 = mybir.dt.float32
F32R = mybir.dt.float32r
BF16 = mybir.dt.bfloat16
U32 = mybir.dt.uint32
ALU = mybir.AluOpType
ACT = mybir.ActivationFunctionType
AX_X = mybir.AxisListType.X

P = 128
BATCH, SEQ, D = 16, 1024, 512
TOK = BATCH * SEQ
KD = D // P
H, HD, NS, R = 16, 32, 16, 16
DI = H * HD
KI = DI // P
CH = 64
ST = 256
NST = TOK // ST
STB = SEQ // ST
HB = 8
NG = H // 4
NE, SETS, ES = 32, 4, 32
EX = NE * SETS
GRP = 32
NQ = EX // 4
LN_EPS, RMS_EPS = 1e-5, 1e-6
TIE = np.arange(GRP, dtype=np.float32) * (np.float32(1e-6) / np.float32(GRP - 1))

C_B, C_DT, C_C, C_L = 0, H * NS, H * NS + H, 2 * H * NS + H
TCOLS = C_L + EX

GB = 64
GT = GB * GRP // P
NGB = TOK // (GB * GRP)
SG = 32
STL = SG * GRP // P
NSB = TOK // (SG * GRP)


def wait(eng, sem, value):
    if not isinstance(value, int) or value > 0:
        eng.wait_ge(sem, value)


def attention_phase(nc, io, keep):
    with ExitStack() as ctx:
        def sb(name, shape, dt=F32):
            return ctx.enter_context(nc.sbuf_tensor(name, shape, dt))

        def sem(name):
            return ctx.enter_context(nc.semaphore(name))

        bank = [ctx.enter_context(nc.psum_tensor(f"a_bank{i}", [P, 512], F32)) for i in range(8)]
        XN_OUT, PROJ0, PROJ1, TBC, SC0, SC1, YB, MISC = range(8)

        wd = [sb(f"wd{n}", [P, KD, 2 * DI], F32R) for n in "hl"]
        wt = [sb(f"wt{n}", [P, KD, TCOLS], F32R) for n in "hl"]
        wo = [sb(f"wo{n}", [P, KI, D], F32R) for n in "hl"]
        stage = sb("stage", [P, 2, KI * D])
        wlow = sb("wlow", [R, D])
        dtw = sb("dtw", [R, H])
        ident = sb("a_ident", [P, P])
        umat = sb("umat", [P, P])
        wmat = sb("wmat", [P, 4])
        mask = sb("mask", [P, CH], U32)
        hsel = sb("hsel", [P, HB])
        hsel4 = sb("hsel4", [P, 4])
        hexp = sb("hexp", [P, NG, P])
        ones = sb("ones", [P, 1])
        inv_di = sb("inv_di", [P, 1])
        mhalf = sb("mhalf", [P, 1])
        ln_eps = sb("ln_eps", [P, 1])
        rms_eps = sb("rms_eps", [P, 1])
        tie = sb("tie", [P, 1])
        a_row = sb("a_row", [P, H])
        dtb_row = sb("dtb_row", [P, H])
        bc_row = sb("bc_row", [P, EX])
        dcol = sb("dcol", [P, KI])
        nwcol = sb("nwcol", [P, KI])
        x = sb("x", [P, 2 * STB, D])
        bst = sb("bst", [P, 2, 6])
        mv = sb("mv", [P, 2, 2])
        ve = sb("ve", [P, 2])
        xn = sb("xn", [P, 2, D])
        xnT = [[sb(f"xnT{n}{b}", [P, KD, ST], F32R) for n in "hl"] for b in range(2)]
        raw = sb("raw", [P, 2, 2, TCOLS])
        v = sb("v", [P, 2, H])
        relu = sb("relu", [P, 2, H])
        vabs = sb("vabs", [P, 2, H])
        ex = sb("ex", [P, 2, H])
        u1 = sb("u1", [P, 2, H])
        lnu = sb("lnu", [P, 2, H])
        rcu = sb("rcu", [P, 2, H])
        lost = sb("lost", [P, 2, H])
        dt = sb("dt", [P, 2, H])
        dA = sb("dA", [P, 2, H])
        e1 = sb("e1", [P, 2, H])
        e2 = sb("e2", [P, 2, H])
        logs = sb("logs", [P, 8])
        mg = sb("mg", [P, 2, NG, 8])
        lb = sb("lb", [P, 2, EX])
        gmax = sb("gmax", [P, ST // GRP])
        permT = sb("permT", [P, 2, ST], BF16)
        BCT = sb("BCT", [P, 4, P])
        cexp = sb("cexp", [P, 2, 2, HB, CH])
        xs = [sb(f"xs{c}", [P, H, HD]) for c in range(2)]
        scan_in = [sb(f"scan_in{c}", [P, H, CH]) for c in range(2)]
        xT = sb("xT", [P, 2, KI, ST])
        sz = sb("sz", [P, 2, KI, ST])
        gs = sb("gs", [P, NG, 2 * HD])
        yv = sb("yv", [P, KI, P])
        yz = sb("yz", [P, KI, P])
        sq = sb("sq", [P, KI, P])
        sq2 = sb("sq2", [P, 2, P])
        ysq = sb("ysq", [P, 2, P])
        yg = [sb(f"yg{n}", [P, 2, KI, P], F32R) for n in "hl"]
        ms = sb("ms", [P, 2])
        rms = sb("rms", [P, 2])
        res = sb("res", [P, 2, D])

        const_in = sem("const_in")
        w_in = [sem(f"w_in{i}") for i in range(2)]
        w_hi = sem("w_hi")
        w_lo = sem("w_lo")
        wdt_ps = sem("wdt_ps")
        wdt_hi = sem("wdt_hi")
        wdt_lo = sem("wdt_lo")
        zeroed = sem("zeroed")
        a_ready = sem("a_ready")
        x_in = [sem(f"x_in{i}") for i in range(2 * STB)]
        ln = sem("ln")
        ln_pool = sem("ln_pool")
        kept = sem("kept")
        xn_ready = sem("xn_ready")
        xnT_ps = sem("xnT_ps")
        xnT_hi = sem("xnT_hi")
        xnT_lo = sem("xnT_lo")
        tok_ps = sem("tok_ps")
        tok_raw = sem("tok_raw")
        sp = sem("sp")
        sp_act = sem("sp_act")
        small_ps = sem("small_ps")
        small_cp = sem("small_cp")
        dA_ready = sem("dA_ready")
        e2_ready = sem("e2_ready")
        mg_ps = sem("mg_ps")
        mg_ready = sem("mg_ready")
        scaled = sem("scaled")
        lbs = sem("lbs")
        lT_ps = sem("lT_ps")
        pm = sem("pm")
        pm_out = [sem(f"pm_out{i}") for i in range(2)]
        d_ps = sem("d_ps")
        d_cp = sem("d_cp")
        tbc_ps = sem("tbc_ps")
        bt_cp = sem("bt_cp")
        cexp_cp = sem("cexp_cp")
        tx_ps = sem("tx_ps")
        xtok_cp = sem("xtok_cp")
        sc_ps = [sem(f"sc_ps{f}") for f in range(2)]
        mt_cp = sem("mt_cp")
        st_ps = sem("st_ps")
        st_add = sem("st_add")
        cs_cp = [sem(f"cs_cp{c}") for c in range(2)]
        cs_low = sem("cs_low")
        g_ready = sem("g_ready")
        scan0 = sem("scan0")
        y_ps = sem("y_ps")
        yv_cp = sem("yv_cp")
        yz_cp = sem("yz_cp")
        sq_cp = sem("sq_cp")
        ysum = sem("ysum")
        yg_hi = sem("yg_hi")
        yg_lo = sem("yg_lo")
        rms_ps = sem("rms_ps")
        rms_cp = sem("rms_cp")
        rms_pool = sem("rms_pool")
        o_ps = sem("o_ps")
        res_cp = sem("res_cp")
        res_out = [sem(f"res_out{i}") for i in range(2)]

        x_dram = io["x"].rearrange("(t p) d -> t p d", p=P)
        part_dram = keep["part"].rearrange("(t p) d -> t p d", p=P)
        perm_dram = keep["permT"].rearrange("e (s t) -> s e t", t=ST)

        stages = []
        for k in range(0, KD, 2):
            stages.append((io["w_tok"][:, k:k + 2, :], None))
        for k in range(0, KD, 2):
            stages.append((io["w_dz"][:, k:k + 2, :], [w[:, k:k + 2, :] for w in wd]))
        stages.append((io["w_out"], [w[:, :, :] for w in wo]))

        def stage_view(n):
            src = stages[n][0]
            return stage[:, n % 2, 0:src.shape[1] * src.shape[2]].rearrange("p (k c) -> p k c", k=src.shape[1])

        def stage_parts(n):
            if stages[n][1] is not None:
                return [(stage_view(n), *stages[n][1])]
            k = 2 * n
            s = stage_view(n)
            nb = C_DT - C_B
            return [(s[:, :, 0:nb], *[w[:, k:k + 2, C_B:C_DT] for w in wt]),
                    (s[:, :, nb:], *[w[:, k:k + 2, C_C:TCOLS] for w in wt])]

        consts = [(ident, "ident"), (umat, "umat"), (wmat, "wmat"), (mask, "mask"), (hsel, "hsel"), (hsel4, "hsel4"),
                  (hexp, "hexp"), (tie, "tie"), (dcol, "dcol"), (nwcol, "nwcol"), (wlow, "w_dtlow"), (dtw, "dt_wT")]
        rows = [(a_row, "a_log"), (dtb_row, "dt_b"), (bc_row, "bc")]
        NCONST = 16 * (len(consts) + len(rows))

        SP = 7

        def valid(b, q):
            return not isinstance(b, int) or 0 <= STB * b + q < NST

        def step_of(b, q):
            return STB * b + q, q % STB

        def run_steps(eng, body):
            for q in range(STB):
                body(0, q)
            with eng.Fori(1, BATCH - 1) as b:
                for q in range(STB):
                    body(b, q)
            for q in range(STB):
                body(BATCH - 1, q)
            for q in range(2):
                body(BATCH, q)

        def token_rows(c):
            return slice(CH * c, CH * c + CH)

        def state_rows(c):
            return slice(CH * (1 - c), CH * (1 - c) + CH)

        def c_rows(w):
            return slice(CH * w, CH * w + CH)

        def c_places(c, w):
            return scan_in[c][state_rows(c), :, :].rearrange("p (f w j) i -> p f w j i", f=2, w=2)[:, :, w, :, :]

        def state_view(c):
            return xs[c][state_rows(c), :, :].rearrange("r (g w a) p -> r g w (a p)", g=NG, w=2)

        block = ctx.enter_context(nc.Block())

        @block.sync
        def _(sync):
            for t in range(3):
                sync.dma_start(x[:, t, :], x_dram[t]).then_inc(x_in[t], 16)
            for n, (src, _) in enumerate(stages):
                if n == 2:
                    for dst, name in consts[4:]:
                        sync.dma_start(dst[:], io[name]).then_inc(const_in, 16)
                    for dst, name in rows:
                        sync.dma_start(dst[:], io[name].partition_broadcast(P)).then_inc(const_in, 16)
                if n >= 2:
                    sync.wait_ge(w_lo, n - 1)
                sync.dma_start(stage_view(n), src).then_inc(w_in[n % 2], 16)
            for t in range(3, 4):
                sync.dma_start(x[:, t, :], x_dram[t]).then_inc(x_in[t], 16)

            def body(b, q):
                s, place = step_of(b, q)
                for i in range(2):
                    if i == 1 and valid(b, q):
                        wait(sync, pm, 2 * s + 2)
                        sync.dma_start(perm_dram[s], permT[:, place % 2, :]).then_inc(pm_out[place % 2], 16)
                    if valid(b, q - 2):
                        wait(sync, res_cp, 2 * (s - 2) + i + 1)
                        sync.dma_start(part_dram[2 * (s - 2) + i], res[:, i, :]).then_inc(res_out[i], 16)
                    if valid(b, q + 2):
                        slot = (2 * (place + 2) + i) % (2 * STB)
                        sync.dma_start(x[:, slot, :], x_dram[2 * (s + 2) + i]).then_inc(x_in[slot], 16)

            run_steps(sync, body)
            for i in range(2):
                sync.wait_ge(res_out[i], 16 * NST)
                sync.wait_ge(pm_out[i], 16 * (NST // 2))

        @block.gpsimd
        def _(pool):
            for col, value in ((ones, 1.0), (inv_di, 1.0 / DI), (mhalf, -0.5), (ln_eps, LN_EPS), (rms_eps, RMS_EPS)):
                nc.gpsimd.memset(col[:], value).then_inc(zeroed, 1)
            pool.wait_ge(zeroed, 5)

            def inv_std(n, j):
                wait(pool, ln, 2 * n + 2)
                wait(pool, xn_ready, n - 1)
                nc.gpsimd.tensor_tensor(ve[:, j:j + 1], mv[:, j, 1:2], ln_eps[:], ALU.add).then_inc(ln_pool, 1)
                wait(pool, ln_pool, 2 * n + 1)
                nc.gpsimd.tensor_tensor(mv[:, j, 1:2], ve[:, j:j + 1], mhalf[:], ALU.pow).then_inc(ln_pool, 1)
                wait(pool, ln_pool, 2 * n + 2)
                nc.gpsimd.tensor_copy(keep["stats"][:, n, :], mv[:, j, :]).then_inc(kept, 1)

            def spread_c(n):
                wait(pool, bt_cp, n + 1)
                for w in range(2):
                    own = c_rows(w)
                    src = BCT[own, 2:4, CH:P].unsqueeze(2).to_broadcast([CH, 2, 4, CH])
                    sel = hsel4[own, :].unsqueeze(1).unsqueeze(3).to_broadcast([CH, 2, 4, CH])
                    nc.gpsimd.tensor_tensor(c_places(1, w), src, sel, ALU.mult).then_inc((cs_low, cs_cp[1])[w], 1)
                    wait(pool, (cs_low, cs_cp[1])[w], n + 1)

            def y_sums(n, i):
                wait(pool, sq_cp, n + 1)
                nc.gpsimd.tensor_tensor(sq2[:], sq[:, 0:2, :], sq[:, 2:4, :], ALU.add).then_inc(ysum, 1)
                wait(pool, ysum, 2 * n + 1)
                wait(pool, rms_ps, n - 1)
                nc.gpsimd.tensor_tensor(ysq[:, i, :], sq2[:, 0, :], sq2[:, 1, :], ALU.add).then_inc(ysum, 1)

            def inv_rms(n, i):
                wait(pool, rms_cp, n + 1)
                wait(pool, res_cp, n - 1)
                nc.gpsimd.tensor_tensor(ms[:, i:i + 1], ms[:, i:i + 1], rms_eps[:], ALU.add).then_inc(rms_pool, 1)
                wait(pool, rms_pool, 2 * n + 1)
                nc.gpsimd.tensor_tensor(rms[:, i:i + 1], ms[:, i:i + 1], mhalf[:], ALU.pow).then_inc(rms_pool, 1)

            def body(b, q):
                s, place = step_of(b, q)
                par = place % 2
                if valid(b, q + 1):
                    inv_std(2 * (s + 1) + 1, 1)
                if valid(b, q - 1):
                    spread_c(2 * (s - 1))
                if valid(b, q - 2):
                    y_sums(2 * (s - 2) + 1, 1)
                    inv_rms(2 * (s - 2), 0)
                if valid(b, q):
                    def logits(i):
                        n = 2 * s + i
                        wait(pool, tok_raw, 2 * n + 2)
                        wait(pool, lT_ps, s)
                        nc.gpsimd.tensor_tensor(lb[:, i, :], raw[:, par, i, C_L:TCOLS], bc_row[:], ALU.add).then_inc(lbs, 1)
                        wait(pool, lbs, 4 * s + 2 * i + 1)
                        nc.gpsimd.tensor_tensor(lb[:, i, :], lb[:, i, :], tie[:].to_broadcast([P, EX]), ALU.add).then_inc(lbs, 1)
                    wait(pool, tok_raw, 4 * s + 3)
                    for i in range(2):
                        r = nc.gpsimd.tensor_tensor(v[:, i, :], raw[:, par, i, C_DT:C_C], dtb_row[:], ALU.add)
                    r.then_inc(sp, 1)
                    logits(0)
                    one = ones[:].unsqueeze(2).to_broadcast([P, 2, H])
                    wait(pool, sp_act, 5 * s + 3)
                    nc.gpsimd.tensor_tensor(u1[:], ex[:], one, ALU.add).then_inc(sp, 1)
                    wait(pool, sp, SP * s + 2)
                    nc.gpsimd.tensor_tensor(lost[:], u1[:], one, ALU.subtract).then_inc(sp, 1)
                    wait(pool, sp, SP * s + 3)
                    nc.gpsimd.tensor_tensor(lost[:], ex[:], lost[:], ALU.subtract).then_inc(sp, 1)
                    logits(1)
                    wait(pool, sp_act, 5 * s + 5)
                    wait(pool, sp, SP * s + 4)
                    nc.gpsimd.tensor_tensor(lost[:], lost[:], rcu[:], ALU.mult).then_inc(sp, 1)
                    nc.gpsimd.tensor_tensor(dt[:], relu[:], lnu[:], ALU.add).then_inc(sp, 1)
                    wait(pool, sp, SP * s + 6)
                    nc.gpsimd.tensor_tensor(dt[:], dt[:], lost[:], ALU.add).then_inc(sp, 1)
                    wait(pool, sp, SP * s + 7)
                    for i in range(2):
                        r = nc.gpsimd.tensor_tensor(dA[:, i, :], dt[:, i, :], a_row[:], ALU.mult)
                    r.then_inc(dA_ready, 1)
                if valid(b, q + 2):
                    inv_std(2 * (s + 2), 0)
                if valid(b, q - 1):
                    spread_c(2 * (s - 1) + 1)
                if valid(b, q - 1):
                    y_sums(2 * (s - 1), 0)
                if valid(b, q - 2):
                    inv_rms(2 * (s - 2) + 1, 1)
                if valid(b, q):
                    wait(pool, small_cp, 3 * s + 2)
                    nc.gpsimd.tensor_tensor(e2[:], e2[:], dt[:], ALU.mult).then_inc(e2_ready, 1)
                    wait(pool, e2_ready, s + 1)
                    for i in range(2):
                        for c0, e in ((C_C, e1), (C_B, e2)):
                            blk = raw[:, par, i, c0:c0 + H * NS].rearrange("p (h n) -> p h n", n=NS)
                            nc.gpsimd.tensor_tensor(blk, blk, e[:, i, :].unsqueeze(2).to_broadcast([P, H, NS]),
                                                    ALU.mult).then_inc(scaled, 1)

            for t in range(2):
                inv_std(t, t)
            for c in range(2):
                nc.gpsimd.memset(scan_in[c][:], 0.0).then_inc(zeroed, 1)
            nc.gpsimd.memset(logs[:], 0.0).then_inc(zeroed, 1)
            pool.wait_ge(const_in, NCONST)
            pool.wait_ge(a_ready, 1)
            nc.gpsimd.tensor_scalar(a_row[:], a_row[:], -1.0, 1.0, ALU.mult, ALU.mult).then_inc(a_ready, 1)
            pool.wait_ge(zeroed, 8)
            pool.wait_ge(a_ready, 2)
            inv_std(2, 0)
            run_steps(pool, body)

        @block.scalar
        def _(act):
            def hi_xn(n, b, i):
                wait(act, xnT_ps, n + 1)
                nc.scalar.copy(xnT[b][0][:, :, i * P:(i + 1) * P], bank[XN_OUT][:].rearrange("p (k t) -> p k t", k=KD)).then_inc(xnT_hi, 1)

            for dst, name in consts[:4]:
                act.dma_start(dst[:], io[name]).then_inc(const_in, 16)
            nc.scalar.preload_act_table_set("natural_log_exp_and_others")
            def stage_hi(n):
                act.wait_ge(w_in[n % 2], 16 * (n // 2 + 1))
                for rawp, hi, lo in stage_parts(n):
                    last = nc.scalar.copy(hi, rawp)
                last.then_inc(w_hi, 1)

            for n in range(len(stages) - 1):
                stage_hi(n)
                if n == KD // 2 - 1:
                    act.wait_ge(const_in, NCONST)
                    nc.scalar.activation(a_row[:], a_row[:], ACT.Exp).then_inc(a_ready, 1)
                    act.wait_ge(wdt_ps, 1)
                    nc.scalar.copy(wt[0][:, :, C_DT:C_C], bank[MISC][:, 0:KD * H].rearrange("p (k h) -> p k h", k=KD)).then_inc(wdt_hi, 1)
                    for i in range(2):
                        hi_xn(i, 0, i)

            def scan_copies(n):
                wait(act, tbc_ps, n + 1)
                nc.scalar.copy(BCT[:], bank[TBC][:].rearrange("p (f t) -> p f t", f=4)).then_inc(bt_cp, 1)
                wait(act, tx_ps, n + 1)
                for c in range(2):
                    last = nc.scalar.copy(xs[c][token_rows(c), :, :], bank[MISC][token_rows(c), :].rearrange("p (h d) -> p h d", h=H))
                last.then_inc(xtok_cp, 1)

            def spread_c(n):
                wait(act, bt_cp, n + 1)
                for w in range(2):
                    own, dst = c_rows(w), c_places(0, w)
                    for j in range(4):
                        last = nc.scalar.activation(dst[:, :, j, :], BCT[own, 2:4, 0:CH], ACT.Copy, scale=hsel4[own, j:j + 1])
                last.then_inc(cs_cp[0], 1)

            def y_tail(n, i):
                wait(act, yv_cp, 4 * n + 4)
                wait(act, ysum, 2 * n - 1)
                nc.scalar.activation(sq[:], yv[:], ACT.Square).then_inc(sq_cp, 1)
                wait(act, yz_cp, 4 * n + 4)
                wait(act, o_ps, n - 1)
                nc.scalar.copy(yg[0][:, i, :, :], yz[:]).then_inc(yg_hi, 1)

            def tok_copies(n, par, i):
                wait(act, tok_ps, 2 * n + 1)
                nc.scalar.copy(raw[:, par, i, 0:C_C], bank[PROJ0][:, 0:C_C]).then_inc(tok_raw, 1)
                wait(act, tok_ps, 2 * n + 2)
                nc.scalar.copy(raw[:, par, i, C_C:TCOLS], bank[PROJ1][:, 0:TCOLS - C_C]).then_inc(tok_raw, 1)

            def rms_copy(n, i, col):
                wait(act, rms_ps, n + 1)
                wait(act, rms_pool, 2 * n - 2)
                nc.scalar.copy(ms[:, i:i + 1], bank[MISC][:, col:col + 1]).then_inc(rms_cp, 1)

            def body(b, q):
                s, place = step_of(b, q)
                par = place % 2
                if valid(b, q + 1):
                    hi_xn(2 * (s + 1), 1 - par, 0)
                if valid(b, q - 1):
                    scan_copies(2 * (s - 1))
                if valid(b, q):
                    tok_copies(2 * s, par, 0)
                if valid(b, q - 1):
                    spread_c(2 * (s - 1))
                if valid(b, q - 2):
                    rms_copy(2 * (s - 2), 0, 64)
                    y_tail(2 * (s - 2) + 1, 1)
                if valid(b, q):
                    tok_copies(2 * s + 1, par, 1)
                    nc.scalar.preload_act_table_set("natural_log_exp_and_others")
                    wait(act, sp, SP * s + 1)
                    nc.scalar.activation(vabs[:], v[:], ACT.Abs).then_inc(sp_act, 1)
                    nc.scalar.activation(relu[:], v[:], ACT.Relu).then_inc(sp_act, 1)
                    wait(act, sp_act, 5 * s + 1)
                    nc.scalar.activation(ex[:], vabs[:], ACT.Exp, scale=-1.0).then_inc(sp_act, 1)
                    wait(act, sp, SP * s + 2)
                    nc.scalar.activation(lnu[:], u1[:], ACT.Ln).then_inc(sp_act, 1)
                    wait(act, sp_act, 5 * s + 4)
                    nc.scalar.activation(rcu[:], lnu[:], ACT.Exp, scale=-1.0).then_inc(sp_act, 1)
                if isinstance(s, int) and s == 0:
                    stage_hi(len(stages) - 1)
                if valid(b, q + 1):
                    hi_xn(2 * (s + 1) + 1, 1 - par, 1)
                if valid(b, q - 1):
                    scan_copies(2 * (s - 1) + 1)
                    spread_c(2 * (s - 1) + 1)
                    y_tail(2 * (s - 1), 0)
                if valid(b, q):
                    wait(act, d_ps, 4 * s + 1)
                    nc.scalar.copy(xT[:, par, 0:2, :], bank[PROJ0][:].rearrange("p (m t) -> p m t", m=2)).then_inc(d_cp, 1)
                    wait(act, d_ps, 4 * s + 2)
                    nc.scalar.copy(xT[:, par, 2:4, :], bank[PROJ1][:].rearrange("p (m t) -> p m t", m=2)).then_inc(d_cp, 1)
                    wait(act, small_ps, s + 1)
                    wait(act, scaled, 4 * s)
                    u = bank[MISC][:, 0:2 * H].rearrange("p (i h) -> p i h", i=2)
                    nc.scalar.activation(e1[:], u, ACT.Exp).then_inc(small_cp, 1)
                    nc.scalar.activation(e2[:], u, ACT.Exp, scale=-1.0).then_inc(small_cp, 1)
                    nc.scalar.copy(logs[0:H, :], bank[MISC][0:H, 2 * H:2 * H + 8]).then_inc(small_cp, 1)
                if valid(b, q - 2):
                    rms_copy(2 * (s - 2) + 1, 1, 64)
                if valid(b, q):
                    wait(act, mg_ps, s + 1)
                    nc.scalar.activation(mg[:, par, :, :], bank[MISC][:, 0:8 * NG].rearrange("p (g c) -> p g c", g=NG),
                                         ACT.Exp).then_inc(mg_ready, 1)
                    for j in range(2):
                        wait(act, d_ps, 4 * s + 3 + j)
                        nc.scalar.activation(sz[:, par, 2 * j:2 * j + 2, :],
                                             bank[PROJ0 + j][:].rearrange("p (m t) -> p m t", m=2), ACT.Silu).then_inc(d_cp, 1)

            run_steps(act, body)

        @block.vector
        def _(dve):
            def stage_lo(n):
                dve.wait_ge(w_hi, n + 1)
                for rawp, hi, lo_ in stage_parts(n):
                    last = nc.vector.tensor_tensor(lo_, rawp, hi.bitcast(F32), ALU.subtract)
                last.then_inc(w_lo, 1)

            def stats(n, slot, j):
                wait(dve, x_in[slot[0]], 16 * (slot[1] + 1))
                wait(dve, kept, n - 1)
                wait(dve, xn_ready, n - 1)
                nc.vector.bn_stats(bst[:, j, :], x[:, slot[0], :]).then_inc(ln, 1)

            def finish_stats(n, j):
                nc.vector.bn_aggr(mv[:, j, :], bst[:, j, :]).then_inc(ln, 1)

            def normalize(n, slot, j):
                wait(dve, ln_pool, 2 * n + 2)
                wait(dve, xnT_ps, n - 1)
                nc.vector.tensor_scalar(xn[:, j, :], x[:, slot[0], :], mv[:, j, 0:1], mv[:, j, 1:2],
                                        ALU.subtract, ALU.mult).then_inc(xn_ready, 1)

            def lo(n, b, i):
                wait(dve, xnT_hi, n + 1)
                nc.vector.tensor_tensor(xnT[b][1][:, :, i * P:(i + 1) * P], bank[XN_OUT][:].rearrange("p (k t) -> p k t", k=KD),
                                        xnT[b][0][:, :, i * P:(i + 1) * P].bitcast(F32), ALU.subtract).then_inc(xnT_lo, 1)

            def expand_c(n):
                wait(dve, bt_cp, n + 1)
                for f in range(2):
                    src = BCT[:, 2 + f, :].rearrange("p (c i) -> p c i", c=2)
                    nc.vector.tensor_tensor(cexp[:, f, :, :, :], src.unsqueeze(2).to_broadcast([P, 2, HB, CH]),
                                            hsel[:].unsqueeze(1).unsqueeze(3).to_broadcast([P, 2, HB, CH]),
                                            ALU.mult).then_inc(cexp_cp, 1)

            def mask_scores(n):
                for f in range(2):
                    dve.wait_ge(zeroed, 8)
                    wait(dve, sc_ps[f], n + 1)
                    for c in range(2):
                        rows_ = slice(c * CH, (c + 1) * CH)
                        nc.vector.copy_predicated(scan_in[c][rows_, f * HB:(f + 1) * HB, :],
                                                  mask[rows_, :].unsqueeze(1).to_broadcast([CH, HB, CH]),
                                                  bank[SC0 + f][rows_, :].rearrange("p (h i) -> p h i", h=HB)).then_inc(mt_cp, 1)

            def y_lo(n, i):
                wait(dve, yg_hi, n + 1)
                nc.vector.tensor_tensor(yg[1][:, i, :, :], yz[:], yg[0][:, i, :, :].bitcast(F32), ALU.subtract).then_inc(yg_lo, 1)

            def residual(s2, i, slot):
                n = 2 * s2 + i
                wait(dve, o_ps, n + 1)
                wait(dve, rms_pool, 2 * n + 2)
                wait(dve, res_out[i], 16 * s2)
                nc.vector.scalar_tensor_tensor(res[:, i, :], bank[XN_OUT][:], rms[:, i:i + 1], x[:, slot, :],
                                               ALU.mult, ALU.add).then_inc(res_cp, 1)

            def states(n, i, c, scale0, scale1):
                rows_ = state_rows(c)
                wait(dve, st_ps, n + 1)
                wait(dve, g_ready, 8 * n + 8 + 4 * c)
                nc.vector.tensor_tensor(gs[rows_, :, :], bank[(TBC, MISC)[c]][rows_, 0:NG * 2 * HD].rearrange("p (g c) -> p g c", g=NG),
                                        state_view(c)[:, :, 0, :], ALU.add).then_inc(st_add, 1)
                wait(dve, st_add, 2 * n + 1 + c)
                if c == 1:
                    wait(dve, scan0, n + 1)
                else:
                    wait(dve, y_ps, n)
                for q in range(NG):
                    dst = state_view(1 - c)[:, q, :, :]
                    if scale1 is None:
                        nc.vector.memset(dst, 0.0).then_inc(g_ready, 1)
                    else:
                        nc.vector.tensor_scalar(dst, gs[rows_, q, :].unsqueeze(1).to_broadcast([CH, 2, 2 * HD]),
                                                scale0[rows_, q, :], scale1[rows_, q, :], ALU.mult, ALU.mult).then_inc(g_ready, 1)

            def gate(n, i, par):
                tt = slice(i * P, (i + 1) * P)
                wait(dve, y_ps, n + 1)
                wait(dve, sq_cp, n)
                for m in range(KI):
                    nc.vector.scalar_tensor_tensor(yv[:, m, :], xT[:, par, m, tt], dcol[:, m:m + 1],
                                                   bank[YB][:, m * P:(m + 1) * P], ALU.mult, ALU.add).then_inc(yv_cp, 1)
                wait(dve, yv_cp, 4 * n + 4)
                wait(dve, yg_lo, n)
                for m in range(KI):
                    nc.vector.scalar_tensor_tensor(yz[:, m, :], yv[:, m, :], nwcol[:, m:m + 1], sz[:, par, m, tt],
                                                   ALU.mult, ALU.mult).then_inc(yz_cp, 1)

            def picks(s, par, count):
                wait(dve, lT_ps, s + 1)
                lt = bank[TBC][:, 0:ST].rearrange("p (g t) -> p g t", t=GRP)
                nc.vector.tensor_reduce(gmax[:], lt, AX_X, ALU.max).then_inc(pm, 1)
                wait(dve, pm, 2 * s + 1)
                wait(dve, pm_out[par], 16 * count)
                nc.vector.tensor_tensor(permT[:, par, :].rearrange("p (g t) -> p g t", t=GRP), lt,
                                        gmax[:].unsqueeze(2).to_broadcast([P, ST // GRP, GRP]), ALU.is_equal).then_inc(pm, 1)

            def body(b, q):
                s, place = step_of(b, q)
                par = place % 2

                def slot(dq, i):
                    qq = q + dq
                    return ((2 * qq + i) % (2 * STB), b + qq // STB)

                for i in range(2):
                    nxt_tile = (1, 1) if i == 0 else (2, 0)
                    more = valid(b, q + nxt_tile[0])
                    n_next = 2 * (s + nxt_tile[0]) + nxt_tile[1]
                    if more:
                        stats(n_next, slot(*nxt_tile), nxt_tile[1])
                        wait(dve, ln, 2 * n_next + 1)
                    if valid(b, q + 1):
                        lo(2 * (s + 1) + i, 1 - par, i)
                    if more:
                        finish_stats(n_next, nxt_tile[1])
                    if valid(b, q - 1):
                        expand_c(2 * (s - 1) + i)
                    if i == 1 and valid(b, q - 1):
                        y_lo(2 * (s - 1), 0)
                    if more:
                        normalize(n_next, slot(*nxt_tile), nxt_tile[1])
                    if i == 0 and valid(b, q - 2):
                        y_lo(2 * (s - 2) + 1, 1)
                    if i == 1 and valid(b, q):
                        half = b * (STB // 2) + q // 2
                        picks(s, par, half)
                    if valid(b, q - 1):
                        mask_scores(2 * (s - 1) + i)
                        states(2 * (s - 1) + i, i, 0, mg[:, 1 - par, :, 4 * i + 1:4 * i + 2], mg[:, 1 - par, :, 4 * i + 2:4 * i + 3])
                    if valid(b, q - 2):
                        residual(s - 2, i, slot(-2, i)[0])
                    if valid(b, q - 1):
                        if i == 0:
                            nxt = mg[:, 1 - par, :, 4:5]
                        else:
                            if valid(b, q):
                                wait(dve, mg_ready, s + 1)
                            nxt = None if place == 0 or not valid(b, q) else mg[:, par, :, 0:1]
                        states(2 * (s - 1) + i, i, 1, mg[:, 1 - par, :, 4 * i + 3:4 * i + 4], nxt)
                        gate(2 * (s - 1) + i, i, 1 - par)
                    if isinstance(s, int) and s == 0 and i == 1:
                        stage_lo(len(stages) - 1)

            for c in range(2):
                for q in range(NG):
                    nc.vector.memset(state_view(c)[:, q, :, :], 0.0).then_inc(g_ready, 1)
            for t in range(2):
                stats(t, (t, 0), t)
                dve.wait_ge(ln, 2 * t + 1)
                finish_stats(t, t)
                normalize(t, (t, 0), t)
            for n in range(len(stages) - 1):
                stage_lo(n)
                if n == KD // 2 - 1:
                    dve.wait_ge(wdt_hi, 1)
                    nc.vector.tensor_tensor(wt[1][:, :, C_DT:C_C], bank[MISC][:, 0:KD * H].rearrange("p (k h) -> p k h", k=KD),
                                            wt[0][:, :, C_DT:C_C].bitcast(F32), ALU.subtract).then_inc(wdt_lo, 1)
                    for i in range(2):
                        lo(i, 0, i)
                    stats(2, (2, 0), 0)
                    dve.wait_ge(ln, 5)
                    finish_stats(2, 0)
                    normalize(2, (2, 0), 0)
            run_steps(dve, body)

        @block.tensor
        def _(pe):
            def split_mm(out, lhs, rhs, k, nk):
                for n, (a, c) in enumerate(((0, 0), (0, 1), (1, 0))):
                    last = nc.tensor.matmul(out, lhs[a], rhs[c], start=(k == 0 and n == 0), stop=(k == nk - 1 and n == 2))
                return last

            def transpose_xn(n, j, freed):
                wait(pe, xn_ready, n + 1)
                wait(pe, xnT_lo, n)
                wait(pe, res_cp, freed)
                for k in range(KD):
                    last = nc.tensor.transpose(bank[XN_OUT][:, k * P:(k + 1) * P], xn[:, j, k * P:(k + 1) * P], ident[:])
                last.then_inc(xnT_ps, 1)

            def transpose_bc(n, par, i):
                wait(pe, scaled, 2 * n + 2)
                if i == 0:
                    wait(pe, pm, n + 2)
                wait(pe, st_add, 2 * n)
                for f in range(2):
                    nc.tensor.transpose(bank[TBC][:, f * P:(f + 1) * P], raw[:, par, i, C_B + f * P:C_B + (f + 1) * P], ident[:])
                for f in range(2):
                    last = nc.tensor.transpose(bank[TBC][:, (2 + f) * P:(3 + f) * P], raw[:, par, i, C_C + f * P:C_C + (f + 1) * P], ident[:])
                last.then_inc(tbc_ps, 1)

            def transpose_x(n, s1, par, i):
                wait(pe, d_cp, 4 * s1 + 2)
                if i == 0:
                    wait(pe, mg_ready, s1 + 1)
                for m in range(KI):
                    last = nc.tensor.transpose(bank[MISC][:, m * P:(m + 1) * P], xT[:, par, m, i * P:(i + 1) * P], ident[:])
                last.then_inc(tx_ps, 1)

            def project_tokens(n, b, i, read, count):
                for half, (c0, c1) in enumerate(((0, C_C), (C_C, TCOLS))):
                    wait(pe, read, count - 1 + half)
                    for k in range(KD):
                        last = split_mm(bank[PROJ0 + half][:, 0:c1 - c0], [t[:, k, i * P:(i + 1) * P] for t in xnT[b]],
                                        [w[:, k, c0:c1] for w in wt], k, KD)
                    last.then_inc(tok_ps, 1)

            def project_features(b, j):
                for m in range(2):
                    f = (2 * j + m) * P
                    for k in range(KD):
                        last = split_mm(bank[PROJ0 + j % 2][:, m * ST:(m + 1) * ST], [w[:, k, f:f + P] for w in wd],
                                        [t[:, k, :] for t in xnT[b]], k, KD)
                last.then_inc(d_ps, 1)

            def sum_squares(n, i):
                wait(pe, ysum, 2 * n + 2)
                nc.tensor.matmul(bank[MISC][:, 64:65], ysq[:, i, :], inv_di[:], start=True, stop=True).then_inc(rms_ps, 1)

            def scores(n):
                wait(pe, bt_cp, n + 1)
                wait(pe, cexp_cp, 2 * n + 2)
                for f in range(2):
                    for c in range(2):
                        last = nc.tensor.matmul(bank[SC0 + f][c * CH:(c + 1) * CH, :], BCT[:, f, c * CH:(c + 1) * CH],
                                                cexp[:, f, c, :, :], start=True, stop=True)
                    last.then_inc(sc_ps[f], 1)

            def project_out(n, i):
                if isinstance(n, int) and n == 0:
                    pe.wait_ge(w_lo, len(stages))
                wait(pe, yg_lo, n + 1)
                for k in range(KI):
                    last = split_mm(bank[XN_OUT][:], [y[:, i, k, :] for y in yg], [w[:, k, :] for w in wo], k, KI)
                last.then_inc(o_ps, 1)

            def chunk_states(n, par, i):
                for p in range(H // 2):
                    for c in range(2):
                        base = state_rows(c).start + 32 * (p % 2)
                        last = nc.tensor.matmul(bank[(TBC, MISC)[c]][base:base + 32, (p // 2) * 2 * HD:(p // 2 + 1) * 2 * HD],
                                                raw[token_rows(c), par, i, C_B + 32 * p:C_B + 32 * p + 32],
                                                xs[c][token_rows(c), 2 * p:2 * p + 2, :], start=True, stop=True)
                last.then_inc(st_ps, 1)

            def scan(n):
                wait(pe, mt_cp, 4 * n + 4)
                wait(pe, yv_cp, 4 * n)
                for c in range(2):
                    wait(pe, cs_cp[c], n + 1)
                    wait(pe, g_ready, 8 * n + 8 + 4 * c)
                    for h in range(H):
                        rows_ = slice(32 * (h % 4), 32 * (h % 4) + 32)
                        col = (h // 4) * P + c * CH
                        last = nc.tensor.matmul(bank[YB][rows_, col:col + CH], xs[c][:, h, :], scan_in[c][:, h, :], start=True, stop=True)
                    last.then_inc(scan0 if c == 0 else y_ps, 1)

            def body(b, q):
                s, place = step_of(b, q)
                par = place % 2
                for i in range(2):
                    n1, n2 = 2 * (s - 1) + i, 2 * (s - 2) + i
                    if valid(b, q + 1):
                        transpose_xn(2 * (s + 1) + i, i, n2)
                    if valid(b, q - 1):
                        transpose_bc(n1, 1 - par, i)
                        transpose_x(n1, s - 1, 1 - par, i)
                    if i == 0:
                        if valid(b, q):
                            wait(pe, xnT_lo, 2 * s + 2)
                            project_tokens(2 * s, par, 0, d_cp, 4 * s)
                        if valid(b, q - 2):
                            if valid(b, q - 1):
                                wait(pe, xtok_cp, n1 + 1)
                            else:
                                wait(pe, st_add, 2 * n1)
                            sum_squares(n2, i)
                        if valid(b, q):
                            project_tokens(2 * s + 1, par, 1, tok_raw, 4 * s + 2)
                        if valid(b, q - 1):
                            if valid(b, q - 2):
                                wait(pe, rms_cp, n2 + 1)
                            scores(n1)
                            chunk_states(n1, 1 - par, i)
                        if valid(b, q - 2):
                            if valid(b, q + 1):
                                wait(pe, xnT_lo, 2 * (s + 1) + i + 1)
                            else:
                                wait(pe, res_cp, n2)
                            project_out(n2, i)
                    else:
                        if isinstance(s, int) and s == 0:
                            pe.wait_ge(w_lo, len(stages) - 1)
                        if valid(b, q):
                            wait(pe, tok_raw, 4 * s + 3)
                            project_features(par, 0)
                            wait(pe, tok_raw, 4 * s + 4)
                            project_features(par, 1)
                        if valid(b, q - 1):
                            wait(pe, xtok_cp, n1 + 1)
                        if valid(b, q - 2):
                            if not valid(b, q - 1):
                                wait(pe, rms_cp, n2)
                            sum_squares(n2, i)
                        if valid(b, q):
                            wait(pe, dA_ready, s + 1)
                            for j in range(0, P, 32):
                                nc.tensor.matmul(bank[MISC][j:j + 32, 0:2 * H], umat[:, j:j + 32], dA[:].rearrange("p i h -> p (i h)"),
                                                 start=True, stop=True)
                            for t in range(2):
                                last = nc.tensor.matmul(bank[MISC][0:H, 2 * H + 4 * t:2 * H + 4 * t + 4], dA[:, t, :], wmat[:],
                                                        start=True, stop=True)
                            last.then_inc(small_ps, 1)
                            wait(pe, lbs, 4 * s + 4)
                            if valid(b, q - 1):
                                wait(pe, bt_cp, n1 + 1)
                            for t in range(2):
                                last = nc.tensor.transpose(bank[TBC][:, t * P:(t + 1) * P], lb[:, t, :], ident[:])
                            last.then_inc(lT_ps, 1)
                        if valid(b, q - 1):
                            scores(n1)
                        if valid(b, q):
                            wait(pe, small_cp, 3 * s + 3)
                            if valid(b, q - 2):
                                wait(pe, rms_cp, n2 + 1)
                            for f in range(NG):
                                for j in range(0, P, 32):
                                    last = nc.tensor.matmul(bank[MISC][j:j + 32, f * 8:(f + 1) * 8], hexp[:, f, j:j + 32], logs[:],
                                                            start=True, stop=True)
                            last.then_inc(mg_ps, 1)
                        if valid(b, q - 2):
                            if valid(b, q + 1):
                                wait(pe, xnT_lo, 2 * (s + 1) + i + 1)
                            else:
                                wait(pe, res_cp, n2)
                            project_out(n2, i)
                        if valid(b, q):
                            wait(pe, d_cp, 4 * s + 1)
                            wait(pe, pm, 2 * s + 2)
                            wait(pe, mg_ready, s + 1)
                            project_features(par, 2)
                        elif valid(b, q - 2):
                            wait(pe, rms_cp, n2 + 1)
                        if valid(b, q - 1):
                            chunk_states(n1, 1 - par, i)
                        if valid(b, q):
                            wait(pe, d_cp, 4 * s + 2)
                            project_features(par, 3)
                    if valid(b, q - 1):
                        scan(n1)

            pe.wait_ge(const_in, NCONST)
            for k in range(KD):
                last = nc.tensor.matmul(bank[MISC][:, k * H:(k + 1) * H], wlow[:, k * P:(k + 1) * P], dtw[:], start=True, stop=True)
            last.then_inc(wdt_ps, 1)
            for i in range(2):
                transpose_xn(i, i, 0)
            pe.wait_ge(w_lo, KD // 2)
            pe.wait_ge(wdt_lo, 1)
            pe.wait_ge(zeroed, 8)
            run_steps(pe, body)


def gather_phase(nc, io, keep):
    with ExitStack() as ctx:
        def sb(name, shape, dt=F32):
            return ctx.enter_context(nc.sbuf_tensor("g_" + name, shape, dt))

        def sem(name):
            return ctx.enter_context(nc.semaphore("g_" + name))

        pick_bank = [ctx.enter_context(nc.psum_tensor(f"g_pick{i}", [P, 512], F32)) for i in range(4)]
        acc_bank = [ctx.enter_context(nc.psum_tensor(f"g_acc{i}", [P, 512], F32)) for i in range(4)]
        GPT = P // GRP
        QB = NQ // 4

        w1 = sb("w1", [P, KD, EX, ES])
        b1 = sb("b1", [P, NQ])
        ident = sb("ident", [P, P], BF16)
        ident32 = sb("ident32", [P, P])
        permT = sb("permT", [P, GT, P], BF16)
        perm = sb("perm", [P, GT, EX, GPT], F32R)
        x = [sb(f"x{i}", [P, GT, P]) for i in range(2)]
        stat = sb("stat", [P, GT, 2])
        xh = sb("xh", [P, GT, P], F32R)
        xl = sb("xl", [P, GT, P], F32R)
        picked = [sb(f"picked{i}", [P, EX, GB]) for i in range(2)]
        inner = sb("inner", [P, 2, NQ, GB // 2])

        small_in = sem("small_in")
        w1_in = [sem(f"w1_in{k}") for k in range(KD)]
        x_in = [sem(f"x_in{i}") for i in range(2)]
        perm_in = sem("perm_in")
        zeroed = sem("zeroed")
        ident_ready = sem("ident_ready")
        stat_cp = sem("stat_cp")
        centred = sem("centred")
        xn_ready = sem("xn_ready")
        hi_ready = sem("hi_ready")
        lo_ready = sem("lo_ready")
        perm_ps = sem("perm_ps")
        perm_cp = [sem(f"perm_cp{i}") for i in range(2)]
        pick_ps = sem("pick_ps")
        pick_cp = [sem(f"pick_cp{i}") for i in range(2)]
        acc_ps = sem("acc_ps")
        acc_cp = [sem(f"acc_cp{i}") for i in range(2)]
        inner_out = sem("inner_out")

        x_dram = io["x"].rearrange("(b t p) (k c) -> b k p t c", p=P, t=GT, c=P)
        perm_dram = keep["permT"].rearrange("e (b t c) -> b e t c", t=GT, c=P)
        inner_dram = keep["inner"]

        def run_batches(eng, body):
            body(0, False)
            with eng.Fori(1, NGB - 1) as b:
                body(b, False)
            body(NGB - 1, True)

        block = ctx.enter_context(nc.Block())

        @block.sync
        def _(sync):
            def load_x(b, k):
                wait(sync, lo_ready, 2 * (4 * b + k - 1))
                sync.dma_start(x[k % 2][:], x_dram[b, k]).then_inc(x_in[k % 2], 16)

            sync.dma_start(permT[:], perm_dram[0]).then_inc(perm_in, 16)
            sync.dma_start(ident32[:], io["ident"]).then_inc(small_in, 16)
            sync.dma_start(b1[:], io["b1"]).then_inc(small_in, 16)
            sync.dma_start(x[0][:], x_dram[0, 0]).then_inc(x_in[0], 16)
            def load_w1(k):
                sync.dma_start(w1[:, k, :, :], io["w1"][:, k, :, :]).then_inc(w1_in[k], 16)

            sync.wait_ge(x_in[0], 16)
            sync.dma_start(x[1][:], x_dram[0, 1]).then_inc(x_in[1], 16)
            load_w1(0)
            def body(b, last):
                first = isinstance(b, int) and b == 0
                load_x(b, 2)
                if first:
                    sync.wait_ge(w1_in[0], 16)
                    load_w1(1)
                    sync.wait_ge(w1_in[1], 16)
                    load_w1(2)
                load_x(b, 3)
                if first:
                    sync.wait_ge(w1_in[2], 16)
                    load_w1(3)
                if not last:
                    sync.wait_ge(perm_ps, b + 1)
                    sync.dma_start(permT[:], perm_dram[b + 1]).then_inc(perm_in, 16)
                    load_x(b + 1, 0)
                    load_x(b + 1, 1)

            run_batches(sync, body)
            sync.wait_ge(inner_out, 2 * 16 * NGB)

        @block.gpsimd
        def _(pool):
            nc.gpsimd.memset(perm[:, 0:GT // 2, :, :].bitcast(F32), 0.0).then_inc(zeroed, 1)

            def normalize(b, k):
                n = 4 * b + k
                if k == 0:
                    wait(pool, xn_ready, n)
                    nc.gpsimd.tensor_copy(stat[:], keep["stats"][:, GT * b:GT * b + GT, :]
                                          if isinstance(b, int) else keep["stats"][:, bass.ds(GT * b, GT), :]).then_inc(stat_cp, 1)
                    pool.wait_ge(stat_cp, b + 1)
                pool.wait_ge(x_in[k % 2], 16 * (2 * b + k // 2 + 1))
                mean, inv = (stat[:, :, j:j + 1].to_broadcast([P, GT, P]) for j in range(2))
                nc.gpsimd.tensor_tensor(x[k % 2][:], x[k % 2][:], mean, ALU.subtract).then_inc(centred, 1)
                pool.wait_ge(centred, n)
                nc.gpsimd.tensor_tensor(x[k % 2][:], x[k % 2][:], inv, ALU.mult).then_inc(xn_ready, 1)

            def body(b, last):
                normalize(b, 2)
                normalize(b, 3)
                if not last:
                    normalize(b + 1, 0)
                    normalize(b + 1, 1)

            nc.gpsimd.tensor_copy(stat[:], keep["stats"][:, 0:GT, :]).then_inc(stat_cp, 1)
            pool.wait_ge(stat_cp, 1)
            pool.wait_ge(xn_ready, 1)
            normalize(0, 1)
            run_batches(pool, body)

        def tiles_of(h):
            return slice(h * GT // 2, (h + 1) * GT // 2)

        def quadrants(bank_index):
            for r in range(GPT):
                rows_ = slice(GRP * r, GRP * r + GRP)
                src = pick_bank[bank_index][:].bitcast(BF16).rearrange("p (t e) -> p t e", t=GT // 2)
                yield perm[rows_, tiles_of(bank_index), :, r], src[rows_, :, :]

        def picked_view(k, t):
            return picked[k % 2][:, :, GPT * t:GPT * t + GPT]

        def pick_view(t):
            return pick_bank[t % 4][:].rearrange("p (e n) -> p e n", n=GPT)

        def inner_view(q):
            return inner[:, :, q, :]

        def acc_view(q):
            return acc_bank[q // QB][:, (q % QB) * GB:(q % QB + 1) * GB].rearrange("p (h n) -> p h n", h=2)

        @block.scalar
        def _(act):
            nc.scalar.preload_act_table_set("natural_log_exp_and_others")

            def split_hi(b, k):
                n = 4 * b + k
                act.wait_ge(xn_ready, n + 1)
                for h in range(2):
                    if h == 0:
                        wait(act, pick_ps, 16 * n)
                    nc.scalar.copy(xh[:, tiles_of(h), :], x[k % 2][:, tiles_of(h), :]).then_inc(hi_ready, 1)

            def copy_picks(b):
                wait(act, perm_ps, b + 1)
                for dst, src in quadrants(0):
                    r = nc.scalar.copy(dst, src)
                r.then_inc(perm_cp[0], 1)

            def copy_picked(b, k):
                for t in range(0, GT, 2):
                    act.wait_ge(pick_ps, 16 * (4 * b + k) + t + 1)
                    nc.scalar.copy(picked_view(k, t), pick_view(t)).then_inc(pick_cp[0], 1)

            def apply_relu(b):
                wait(act, inner_out, 32 * b)
                for j in range(2):
                    act.wait_ge(acc_ps, 4 * b + j + 1)
                    for q in range(QB * j, QB * j + QB):
                        r = nc.scalar.activation(inner_view(q), acc_view(q), ACT.Relu, bias=b1[:, q:q + 1])
                    r.then_inc(acc_cp[0], 1)

            def store_inner(b):
                for i in range(2):
                    act.wait_ge(acc_cp[i], 2 * b + 2)
                for h in range(2):
                    act.dma_start(inner_dram[2 * b + h], inner[:, h, :, :]).then_inc(inner_out, 16)

            def body(b, last):
                copy_picked(b, 1)
                split_hi(b, 2)
                copy_picked(b, 2)
                split_hi(b, 3)
                copy_picked(b, 3)
                if not last:
                    copy_picks(b + 1)
                    split_hi(b + 1, 0)
                    copy_picked(b + 1, 0)
                    split_hi(b + 1, 1)
                apply_relu(b)
                store_inner(b)

            act.wait_ge(small_in, 32)
            nc.scalar.copy(ident[:], ident32[:]).then_inc(ident_ready, 1)
            act.wait_ge(zeroed, 2)
            copy_picks(0)
            split_hi(0, 0)
            copy_picked(0, 0)
            split_hi(0, 1)
            run_batches(act, body)

        @block.vector
        def _(dve):
            def split_lo(b, k):
                n = 4 * b + k
                for h in range(2):
                    dve.wait_ge(hi_ready, 2 * n + h + 1)
                    nc.vector.tensor_tensor(xl[:, tiles_of(h), :], x[k % 2][:, tiles_of(h), :],
                                            xh[:, tiles_of(h), :].bitcast(F32), ALU.subtract).then_inc(lo_ready, 1)

            def copy_picks(b):
                wait(dve, perm_ps, b + 1)
                for dst, src in quadrants(1):
                    r = nc.vector.tensor_copy(dst, src)
                r.then_inc(perm_cp[1], 1)

            def copy_picked(b, k):
                for t in range(1, GT, 2):
                    dve.wait_ge(pick_ps, 16 * (4 * b + k) + t + 1)
                    nc.vector.tensor_copy(picked_view(k, t), pick_view(t)).then_inc(pick_cp[1], 1)

            def apply_relu(b):
                wait(dve, inner_out, 32 * b)
                for j in range(2, 4):
                    dve.wait_ge(acc_ps, 4 * b + j + 1)
                    for q in range(QB * j, QB * j + QB):
                        r = nc.vector.tensor_scalar(inner_view(q), acc_view(q), b1[:, q:q + 1], 0.0, ALU.add, ALU.max)
                    r.then_inc(acc_cp[1], 1)

            def body(b, last):
                copy_picked(b, 1)
                split_lo(b, 2)
                copy_picked(b, 2)
                split_lo(b, 3)
                copy_picked(b, 3)
                if not last:
                    copy_picks(b + 1)
                    split_lo(b + 1, 0)
                    copy_picked(b + 1, 0)
                    split_lo(b + 1, 1)
                apply_relu(b)

            nc.vector.memset(perm[:, GT // 2:, :, :].bitcast(F32), 0.0).then_inc(zeroed, 1)
            dve.wait_ge(small_in, 32)
            dve.wait_ge(x_in[0], 16)
            for t in range(GT):
                r = nc.vector.tensor_scalar(x[0][:, t, :], x[0][:, t, :], keep["stats"][:, t, 0:1], keep["stats"][:, t, 1:2],
                                            ALU.subtract, ALU.mult)
            r.then_inc(xn_ready, 1)
            dve.wait_ge(zeroed, 2)
            copy_picks(0)
            split_lo(0, 0)
            copy_picked(0, 0)
            split_lo(0, 1)
            run_batches(dve, body)

        @block.tensor
        def _(pe):
            def transpose_picks(b, n):
                pe.wait_ge(perm_in, 16 * (b + 1))
                for i in range(2):
                    wait(pe, pick_cp[i], 8 * n)
                for t in range(GT):
                    dst = pick_bank[t // (GT // 2)][:].bitcast(BF16)
                    c = (t % (GT // 2)) * P
                    last = nc.tensor.transpose(dst[:, c:c + P], permT[:, t, :], ident[:])
                last.then_inc(perm_ps, 1)

            def pick(b, k):
                n = 4 * b + k
                if k == 0:
                    for i in range(2):
                        pe.wait_ge(perm_cp[i], b + 1)
                for t in range(GT):
                    if t % (GT // 2) == 0:
                        pe.wait_ge(lo_ready, 2 * n + t // (GT // 2) + 1)
                    wait(pe, pick_cp[t % 2], 8 * n + t // 2 - 1)
                    rhs = perm[:, t, :, :]
                    nc.tensor.matmul(pick_bank[t % 4][:], xh[:, t, :], rhs, start=True, stop=False)
                    nc.tensor.matmul(pick_bank[t % 4][:], xl[:, t, :], rhs, start=False, stop=True).then_inc(pick_ps, 1)

            def apply_w1(b, k):
                n = 4 * b + k
                if not isinstance(b, int) or b == 0:
                    pe.wait_ge(w1_in[k], 16)
                for i in range(2):
                    pe.wait_ge(pick_cp[i], 8 * (n + 1))
                for q in range(NQ):
                    j, c = q // QB, (q % QB) * GB
                    if k == 0 and q % QB == 0:
                        wait(pe, acc_cp[j // 2], 2 * b - 1 + j % 2)
                    for e in range(4):
                        last = nc.tensor.matmul(acc_bank[j][ES * e:ES * e + ES, c:c + GB], w1[:, k, 4 * q + e, :],
                                                picked[k % 2][:, 4 * q + e, :], start=(k == 0 and q % QB == 0),
                                                stop=(k == KD - 1), skip_group_check=True)
                    if k == KD - 1 and q % QB == QB - 1:
                        last.then_inc(acc_ps, 1)

            def body(b, last):
                pick(b, 1)
                apply_w1(b, 0)
                pick(b, 2)
                apply_w1(b, 1)
                pick(b, 3)
                if not last:
                    transpose_picks(b + 1, 4 * b + 4)
                apply_w1(b, 2)
                if not last:
                    pick(b + 1, 0)
                apply_w1(b, 3)

            pe.wait_ge(ident_ready, 1)
            transpose_picks(0, 0)
            pick(0, 0)
            run_batches(pe, body)


def scatter_phase(nc, io, keep):
    with ExitStack() as ctx:
        def sb(name, shape, dt=F32):
            return ctx.enter_context(nc.sbuf_tensor("s_" + name, shape, dt))

        def sem(name):
            return ctx.enter_context(nc.semaphore("s_" + name))

        w2_bank = [ctx.enter_context(nc.psum_tensor(f"s_w2_{i}", [P, 512], F32)) for i in range(4)]
        rt_bank = [ctx.enter_context(nc.psum_tensor(f"s_rt{i}", [P, 512], F32)) for i in range(2)]
        out_bank = [ctx.enter_context(nc.psum_tensor(f"s_sum{i}", [P, 512], F32)) for i in range(2)]
        GPT = P // GRP
        QG = NQ // STL
        STEPS = NSB * KD

        w2 = sb("w2", [P, NQ, D])
        b2 = sb("b2", [P, KD, EX])
        ident = sb("ident", [P, P])
        inner = [sb(f"inner{i}", [P, NQ, SG]) for i in range(2)]
        inner4 = [sb(f"inner4_{i}", [P, NQ, SG, 4]) for i in range(2)]
        permT = [sb(f"permT{i}", [P, SG * GRP], BF16) for i in range(2)]
        perm = [sb(f"perm{i}", [P, SG * GRP]) for i in range(2)]
        resT = [sb(f"resT{i}", [P, SG, EX]) for i in range(2)]
        res = sb("res", [P, 4, GPT, P])
        ones = sb("ones", [P, 1])
        part = [sb(f"part{i}", [P, STL, P]) for i in range(2)]
        out = [sb(f"out{i}", [P, STL, P]) for i in range(2)]

        small_in = sem("small_in")
        w2_first = [sem(f"w2_first{j}") for j in range(4)]
        w2_in = [sem(f"w2_in{k}") for k in range(KD)]
        inner_in = [sem(f"inner_in{i}") for i in range(2)]
        perm_in = [sem(f"perm_in{i}") for i in range(2)]
        part_in = [sem(f"part_in{i}") for i in range(2)]
        zeroed = sem("zeroed")
        zeroed_first = sem("zeroed_first")
        inner_first = sem("inner_first")
        inner_ready = sem("inner_ready")
        perm_ready = sem("perm_ready")
        w2_ps = sem("w2_ps")
        res_ready = sem("res_ready")
        res_ps = sem("res_ps")
        res_cp = sem("res_cp")
        out_ps = sem("out_ps")
        out_cp = sem("out_cp")
        out_done = [sem(f"out_done{i}") for i in range(2)]

        part_dram = keep["part"].rearrange("(b t p) (k c) -> b k p t c", p=P, t=STL, c=P)
        out_dram = io["out"].rearrange("(b t p) (k c) -> b k p t c", p=P, t=STL, c=P)
        perm_dram = keep["permT"].rearrange("e (b c) -> b e c", c=SG * GRP)

        def run_batches(eng, body):
            for i in range(2):
                body(0, i)
            with eng.Fori(1, NSB // 2 - 1) as pair:
                for i in range(2):
                    body(pair, i)
            for i in range(2):
                body(NSB // 2 - 1, i)

        def is_first(pair, i, k, steps=1):
            return isinstance(pair, int) and KD * (2 * pair + i) + k < steps

        def is_last(pair, i, batches):
            return isinstance(pair, int) and 2 * pair + i + batches >= NSB

        block = ctx.enter_context(nc.Block())

        @block.sync
        def _(sync):
            def load_part(b, k):
                sync.dma_start(part[k % 2][:], part_dram[b, k]).then_inc(part_in[k % 2], 16)

            def load_batch(b, i):
                sync.dma_start(inner[i][:], keep["inner"][b]).then_inc(inner_in[i], 16)
                sync.dma_start(permT[i][:], perm_dram[b]).then_inc(perm_in[i], 16)

            def store(b, k):
                sync.dma_start(out_dram[b, k], out[k % 2][:]).then_inc(out_done[k % 2], 16)

            sync.dma_start(inner[0][:], keep["inner"][0]).then_inc(inner_in[0], 16)
            for j in range(4):
                quads = slice(j * NQ // 4, (j + 1) * NQ // 4)
                sync.dma_start(w2[:, quads, 0:P], io["w2"][:, quads, 0:P]).then_inc(w2_first[j], 16)
                if j == 0:
                    sync.dma_start(ident[:], io["ident"]).then_inc(small_in, 16)
                    sync.dma_start(b2[:], io["b2"]).then_inc(small_in, 16)
            sync.dma_start(permT[0][:], perm_dram[0]).then_inc(perm_in[0], 16)
            for k in range(1, KD):
                sync.dma_start(w2[:, :, k * P:(k + 1) * P], io["w2"][:, :, k * P:(k + 1) * P]).then_inc(w2_in[k], 16)
                if k == 1:
                    load_part(0, 0)
                    load_part(0, 1)
            load_batch(1, 1)

            def body(pair, i):
                b = 2 * pair + i
                for k in range(KD):
                    if not is_first(pair, i, k):
                        sync.wait_ge(out_cp, 2 * (KD * b + k))
                        if k < KD - 1:
                            load_part(b, k + 1)
                        elif not is_last(pair, i, 1):
                            load_part(b + 1, 0)
                        store(*((b, k - 1) if k else (b - 1, KD - 1)))
                    if k == 1 and not is_last(pair, i, 2):
                        sync.wait_ge(inner_ready, b + 1)
                        sync.wait_ge(perm_ready, b + 1)
                        load_batch(b + 2, i)

            run_batches(sync, body)
            sync.wait_ge(out_cp, 2 * STEPS)
            store(NSB - 1, KD - 1)
            for i in range(2):
                sync.wait_ge(out_done[i], 16 * STEPS // 2)

        @block.gpsimd
        def _(pool):
            def spread_picks(pair, i):
                b = 2 * pair + i
                pool.wait_ge(perm_in[i], 16 * (pair + 1))
                wait(pool, out_ps, STL * KD * (b - 1))
                nc.gpsimd.tensor_tensor(perm[i][:], permT[i][:], ones[:].to_broadcast([P, SG * GRP]), ALU.mult).then_inc(perm_ready, 1)

            def spread(pair, i):
                b = 2 * pair + i
                wait(pool, perm_ready, b)
                pool.wait_ge(inner_in[i], 16 * (pair + 1))
                wait(pool, w2_ps, STL * KD * (b - 1))
                for e in range(4):
                    rows_ = slice(ES * e, ES * e + ES)
                    r = nc.gpsimd.tensor_tensor(inner4[i][rows_, :, :, e], inner[i][rows_, :, :],
                                                ones[rows_].unsqueeze(2).to_broadcast([ES, NQ, SG]), ALU.mult)
                r.then_inc(inner_ready, 1)

            def body(pair, i):
                if not is_last(pair, i, 1):
                    following = (pair, 1) if i == 0 else (pair + 1, 0)
                    spread(*following)
                    pool.wait_ge(inner_ready, 2 * pair + i + 2)
                    spread_picks(*following)

            nc.gpsimd.memset(ones[:], 1.0).then_inc(zeroed, 1)
            nc.gpsimd.memset(inner4[1][:], 0.0).then_inc(zeroed, 1)
            pool.wait_ge(zeroed, 2)
            spread_picks(0, 0)
            pool.wait_ge(inner_ready, 1)
            run_batches(pool, body)

        @block.scalar
        def _(act):
            def copy_results(m, t):
                act.wait_ge(res_ps, STL * m + t + 1)
                nc.scalar.copy(res[:, t % 4, :, :], rt_bank[t % 2][:].rearrange("p (n d) -> p n d", n=GPT)).then_inc(res_cp, 1)

            def body(pair, i):
                for k in range(KD):
                    if not is_first(pair, i, k):
                        for t in range(STL):
                            copy_results(KD * (2 * pair + i) + k - 1, t)

            act.wait_ge(zeroed_first, 1)
            act.wait_ge(inner_in[0], 16)
            for e in range(2):
                rows_ = slice(ES * e, ES * e + ES)
                r = nc.scalar.copy(inner4[0][rows_, :, :, e], inner[0][rows_, :, :])
            r.then_inc(inner_first, 1)
            run_batches(act, body)
            for t in range(STL):
                copy_results(STEPS - 1, t)

        @block.vector
        def _(dve):
            def add_b2(m, k, t):
                sets = slice(4 * QG * t, 4 * QG * (t + 1))
                dve.wait_ge(w2_ps, STL * m + t + 1)
                nc.vector.tensor_tensor(
                    resT[k % 2][:, :, sets].rearrange("p n (q e) -> p q n e", e=4),
                    w2_bank[t % 4][:].rearrange("p (q n e) -> p q n e", q=QG, e=4),
                    b2[:, k, sets].rearrange("p (q e) -> p q e", e=4).unsqueeze(2).to_broadcast([P, QG, SG, 4]),
                    ALU.add).then_inc(res_ready, 1)

            def write_out(b, m, k, h):
                use = 2 * b + k // 2
                tiles = slice(h * STL // 2, (h + 1) * STL // 2)
                dve.wait_ge(out_ps, STL * m + (h + 1) * STL // 2)
                dve.wait_ge(part_in[k % 2], 16 * (use + 1))
                wait(dve, out_done[k % 2], 16 * use)
                nc.vector.tensor_tensor(out[k % 2][:, tiles, :], out_bank[h][:].rearrange("p (t d) -> p t d", d=P),
                                        part[k % 2][:, tiles, :], ALU.add).then_inc(out_cp, 1)

            def body(pair, i):
                b = 2 * pair + i
                for k in range(KD):
                    m = KD * b + k
                    for t in range(STL):
                        add_b2(m, k, t)
                        if t == 0 and not is_first(pair, i, k, 2):
                            write_out(b, m - 2, k - 2, 1)
                        if t == STL // 2 and not is_first(pair, i, k):
                            write_out(b, m - 1, k - 1, 0)

            nc.vector.memset(inner4[0][:], 0.0).then_inc(zeroed_first, 1)
            dve.wait_ge(zeroed_first, 1)
            dve.wait_ge(inner_in[0], 16)
            for e in range(2, 4):
                rows_ = slice(ES * e, ES * e + ES)
                r = nc.vector.tensor_copy(inner4[0][rows_, :, :, e], inner[0][rows_, :, :])
            r.then_inc(inner_ready, 1)
            dve.wait_ge(small_in, 32)
            run_batches(dve, body)
            write_out(NSB, STEPS - 2, -2, 1)
            write_out(NSB, STEPS - 1, -1, 0)
            write_out(NSB, STEPS - 1, -1, 1)

        @block.tensor
        def _(pe):
            def apply_w2(m, k, t, i):
                wait(pe, res_ready, STL * m + t - 3)
                for j in range(QG):
                    q = QG * t + j
                    last = nc.tensor.matmul(w2_bank[t % 4][:, j * P:(j + 1) * P], w2[:, q, k * P:(k + 1) * P], inner4[i][:, q, :, :],
                                            start=True, stop=True)
                last.then_inc(w2_ps, 1)

            def transpose_results(m, k, t):
                if t == 0:
                    pe.wait_ge(res_ready, STL * (m + 1))
                wait(pe, res_cp, STL * m + t - 1)
                for g in range(GPT):
                    last = nc.tensor.transpose(rt_bank[t % 2][:, g * P:(g + 1) * P], resT[k % 2][:, GPT * t + g, :], ident[:])
                last.then_inc(res_ps, 1)

            def gather_results(b, m, i, k, t):
                h = t // (STL // 2)
                if k == 0 and t == 0:
                    pe.wait_ge(perm_ready, b + 1)
                pe.wait_ge(res_cp, STL * m + t + 1)
                if t % (STL // 2) == 0:
                    wait(pe, out_cp, 2 * m - 1 + h)
                c = (t % (STL // 2)) * P
                for g in range(GPT):
                    tok = (GPT * t + g) * GRP
                    last = nc.tensor.matmul(out_bank[h][GRP * g:GRP * g + GRP, c:c + P], perm[i][:, tok:tok + GRP],
                                            res[:, t % 4, g, :], start=True, stop=True)
                last.then_inc(out_ps, 1)

            def before(b, i, k, steps):
                return (b if k >= steps else b - 1), KD * b + k - steps, (i if k >= steps else 1 - i), (k - steps) % KD

            def finish(b, i, k, t, first2):
                if t > 0:
                    gather_results(*before(b, i, k, 1), t - 1)
                elif not first2:
                    gather_results(*before(b, i, k, 2), STL - 1)
                _, m1, _, k1 = before(b, i, k, 1)
                transpose_results(m1, k1, t)

            def body(pair, i):
                b = 2 * pair + i
                for k in range(KD):
                    if k == 0:
                        pe.wait_ge(inner_ready, b + 1)
                    if is_first(pair, i, k, KD) and k > 0:
                        pe.wait_ge(w2_in[k], 16)
                    for t in range(STL):
                        if is_first(pair, i, k) and t % (STL // 4) == 0:
                            pe.wait_ge(w2_first[t // (STL // 4)], 16)
                        apply_w2(KD * b + k, k, t, i)
                        if not is_first(pair, i, k):
                            finish(b, i, k, t, is_first(pair, i, k, 2))

            pe.wait_ge(small_in, 32)
            pe.wait_ge(inner_first, 1)
            run_batches(pe, body)
            for t in range(STL):
                finish(NSB, 0, 0, t, False)
            gather_results(*before(NSB, 0, 0, 1), STL - 1)


def program(nc, io):
    with nc.sbuf_tensor("token_stats", [P, TOK // P, 2], F32) as stats:
        keep = dict(
            stats=stats,
            part=nc.dram_tensor("part_dram", [TOK, D], F32, kind="Internal").ap(),
            permT=nc.dram_tensor("permT_dram", [EX, TOK], BF16, kind="Internal").ap(),
            inner=nc.dram_tensor("inner_dram", [NSB, P, NQ, SG], F32, kind="Internal").ap(),
        )
        attention_phase(nc, io, keep)
        gather_phase(nc, io, keep)
        scatter_phase(nc, io, keep)


def layout(L0_attn_x, L0_attn_W_in, L0_attn_dt_W, L0_attn_dt_b, L0_attn_A_log, L0_attn_D_param, L0_attn_W_out,
           L0_attn_norm_w, L0_ffn_Wc, L0_ffn_bc, L0_ffn_W1, L0_ffn_b1, L0_ffn_W2, L0_ffn_b2):
    def blocks(w):
        return w.reshape(-1, P, w.shape[1]).transpose(1, 0, 2)

    nxz, nb = 2 * DI, H * NS
    tok_cols = np.concatenate([L0_attn_W_in[nxz:nxz + 2 * nb].T, L0_ffn_Wc.reshape(D, EX)], axis=1)
    tok = np.arange(P)
    same = tok[:, None] // CH == tok[None, :] // CH
    first = tok % CH == 0
    umat = same * ((tok[:, None] <= tok[None, :]) - 0.5 * first[:, None] - 0.5)
    wmat = np.stack([(tok // CH == c) * (0.5 + sign * 0.5 * first) for c in range(2) for sign in (1, -1)], axis=1)
    hexp = np.zeros((P, NG, P))
    for h in range(H):
        hexp[h, h // 4] = tok % CH // NS == h % 4
    return dict(
        x=L0_attn_x.reshape(-1, D),
        w_dz=blocks(L0_attn_W_in[:nxz].T),
        w_tok=blocks(tok_cols),
        w_out=blocks(L0_attn_W_out.T),
        w_dtlow=L0_attn_W_in[nxz + 2 * nb:],
        dt_wT=L0_attn_dt_W.T,
        a_log=L0_attn_A_log, dt_b=L0_attn_dt_b, bc=L0_ffn_bc.reshape(EX),
        dcol=np.repeat(L0_attn_D_param, HD).reshape(KI, P).T,
        nwcol=L0_attn_norm_w.reshape(KI, P).T,
        w1=L0_ffn_W1.reshape(EX, KD, P, ES).transpose(2, 1, 0, 3),
        b1=L0_ffn_b1.reshape(NQ, 4, ES).transpose(1, 2, 0).reshape(P, NQ),
        w2=L0_ffn_W2.reshape(NQ, 4, D, ES).transpose(1, 3, 0, 2).reshape(P, NQ, D),
        b2=L0_ffn_b2.reshape(EX, KD, P).transpose(2, 1, 0),
        ident=np.eye(P, dtype=np.float32),
        umat=umat.astype(np.float32), wmat=wmat.astype(np.float32),
        mask=(np.arange(CH)[None, :] >= (tok % CH)[:, None]).astype(np.uint32),
        hsel=(tok[:, None] // NS == np.arange(HB)[None, :]).astype(np.float32),
        hsel4=(tok[:, None] % CH // NS == np.arange(4)[None, :]).astype(np.float32),
        hexp=hexp.astype(np.float32),
        tie=TIE[tok % GRP].reshape(P, 1),
    )


def kernel(**inputs):
    import concourse.bacc as bacc
    from concourse.bass_utils import run_bass_kernel_spmd

    nc = bacc.Bacc("TRN2", target_bir_lowering=False, num_devices=1)
    arrays, io = {}, {}
    for name, a in layout(**{n: np.asarray(a) for n, a in inputs.items()}).items():
        a = np.ascontiguousarray(a)
        arrays[f"in_{name}_dram"] = a
        io[name] = nc.dram_tensor(f"in_{name}_dram", a.shape, mybir.dt.from_np(a.dtype), kind="ExternalInput").ap()
    io["out"] = nc.dram_tensor("out_0_dram", (TOK, D), F32, kind="ExternalOutput").ap()
    program(nc, io)
    result = run_bass_kernel_spmd(nc, [arrays], core_ids=[0])
    return result.results[0]["out_0_dram"].reshape(BATCH, SEQ, D)
```
